# Optimizing a Trainium2 kernel written in Bass

```python
import numpy as np
import jax
import jax.numpy as jnp

def _softmax(x, axis=-1):
    return jax.nn.softmax(x, axis=axis)

def _gelu(x):
    return jax.nn.gelu(x, approximate=True)

def _silu(x):
    return jax.nn.silu(x)

def _sigmoid(x):
    return jax.nn.sigmoid(x)

def _layernorm(x, axis=-1, eps=1e-05):
    m = jnp.mean(x, axis=axis, keepdims=True)
    v = jnp.var(x, axis=axis, keepdims=True)
    return (x - m) / jnp.sqrt(v + eps)

def _scatter_add(tgt, idx, src, axis=0):
    return tgt.at[idx].add(src)

def _segment_sum(src, seg, n):
    return jax.ops.segment_sum(src, seg, n)
kernel_name = 'mk_flamingo_gated_d1_seqx_r8_c07e05'

def setup_inputs(seed: int=0):
    np.random.seed(seed)
    _w = jnp.asarray

    def _rec_inputs():
        import jax
        import jax.numpy as jnp
        _rk = jax.random.key(seed)
        x = 7.22e-05 + 1 * jax.random.normal(jax.random.fold_in(_rk, 1), (16, 56, 128), jnp.float32)
        _lenS = 56 - jax.random.randint(jax.random.fold_in(_rk, 7), (16,), 0, max(1, 56 // 4) + 1, jnp.int32)
        _lenS2 = 1500 - jax.random.randint(jax.random.fold_in(_rk, 8), (16,), 0, max(1, 1500 // 4) + 1, jnp.int32)
        _ctx_1024P = jax.random.normal(jax.random.fold_in(_rk, 11), (16, 16, 128), jnp.float32)
        _ctx_1024c = jax.random.dirichlet(jax.random.fold_in(_rk, 511), 0.3 * jnp.ones((16,), jnp.float32), (16, 1500))
        _ctx_1024t = jnp.einsum('bsk,bkd->bsd', _ctx_1024c, _ctx_1024P)
        _ctx_1024t = _ctx_1024t * jax.lax.rsqrt(jnp.mean(jnp.square(_ctx_1024t)) + 1e-12) * 0.953939
        ctx_1024 = 4.13588e-05 + 0.999923 * (_ctx_1024t + 0.3 * jax.random.normal(jax.random.fold_in(_rk, 611), (16, 1500, 128), jnp.float32))
        _g = jax.random.normal(jax.random.fold_in(_rk, 9001), (2, 1), jnp.float32)
        _g = jnp.sign(_g) * jnp.maximum(jnp.abs(_g), 1.0) + (_g == 0) * 1.0
        g_xattn = _g[0]
        g_ffn = _g[1]
        return (x, ctx_1024, g_xattn, g_ffn)
    x, ctx_1024, g_xattn, g_ffn = _rec_inputs()

    def _L0_xattn_setup():
        import jax, jax.numpy as jnp
        import numpy as np
        import math
        D_MODEL = 128
        NHEAD = 16
        FACTOR = 1
        B, L = (2, 512)

        def _autocorr_forward(query, key, value, Wq, bq, Wk, bk, Wv, bv, Wo, bo):
            Bq, Lq, d = query.shape
            Lk = key.shape[1]
            H = NHEAD
            Dk = d // H
            Q = (query @ Wq + bq).reshape(Bq, Lq, H, Dk).transpose(0, 2, 1, 3)
            K = (key @ Wk + bk).reshape(Bq, Lk, H, Dk).transpose(0, 2, 1, 3)
            V = (value @ Wv + bv).reshape(Bq, Lk, H, Dk).transpose(0, 2, 1, 3)
            if Lk > Lq:
                K = K[:, :, :Lq, :]
                V = V[:, :, :Lq, :]
            elif Lq > Lk:
                pad = [(0, 0), (0, 0), (0, Lq - Lk), (0, 0)]
                K = jnp.pad(K, pad)
                V = jnp.pad(V, pad)
            Lloc = Lq
            Qf = jnp.fft.rfft(Q, axis=2)
            Kf = jnp.fft.rfft(K, axis=2)
            corr = jnp.fft.irfft(Qf * jnp.conj(Kf), n=Lloc, axis=2)
            corr_mean = corr.mean(axis=-1)
            top_k = min(max(1, int(FACTOR * math.log(Lloc + 1))), Lloc)
            w, idx = jax.lax.top_k(corr_mean, top_k)
            w = jax.nn.softmax(w, axis=-1)
            ar = jnp.arange(Lloc)
            shifted = (ar[None, None, None, :] + idx[..., None]) % Lloc
            rolled = jnp.take_along_axis(V[:, :, None, :, :], shifted[..., None], axis=3)
            out = jnp.einsum('bhk,bhkld->bhld', w, rolled)
            out = out.transpose(0, 2, 1, 3).reshape(Bq, Lq, d)
            return out @ Wo + bo
        key = jax.random.key(seed)
        ks = jax.random.split(key, 12)
        s = 0.02
        inp = {'query': jax.random.normal(ks[0], (B, L, D_MODEL), dtype=jnp.float32), 'key': jax.random.normal(ks[1], (B, L, D_MODEL), dtype=jnp.float32), 'value': jax.random.normal(ks[2], (B, L, D_MODEL), dtype=jnp.float32), 'Wq': jax.random.normal(ks[3], (D_MODEL, D_MODEL), dtype=jnp.float32) * s, 'bq': jnp.zeros((D_MODEL,), dtype=jnp.float32), 'Wk': jax.random.normal(ks[4], (D_MODEL, D_MODEL), dtype=jnp.float32) * s, 'bk': jnp.zeros((D_MODEL,), dtype=jnp.float32), 'Wv': jax.random.normal(ks[5], (D_MODEL, D_MODEL), dtype=jnp.float32) * s, 'bv': jnp.zeros((D_MODEL,), dtype=jnp.float32), 'Wo': jax.random.normal(ks[6], (D_MODEL, D_MODEL), dtype=jnp.float32) * s, 'bo': jnp.zeros((D_MODEL,), dtype=jnp.float32)}
        return inp
    _L0_xattn_all = _L0_xattn_setup()
    _L0_xattn_in = {k: v for k, v in _L0_xattn_all.items() if k in ('Wq', 'bq', 'Wk', 'bk', 'Wv', 'bv', 'Wo', 'bo')}
    del _L0_xattn_all

    def _L0_ffn_setup():
        import jax, jax.numpy as jnp
        import numpy as np
        from jax import lax
        D = 128
        H = 512
        E = 8
        TOPK = 2
        key = jax.random.key(seed)
        ks = jax.random.split(key, 7)
        s = 0.02
        return {'x': jax.random.normal(ks[0], (2, 256, D), dtype=jnp.float32), 'W1': jax.random.normal(ks[1], (E, D, H), dtype=jnp.float32) * s, 'b1': jnp.zeros((E, H), dtype=jnp.float32), 'W2': jax.random.normal(ks[2], (E, H, D), dtype=jnp.float32) * s, 'b2': jnp.zeros((E, D), dtype=jnp.float32), 'Wr': jax.random.normal(ks[3], (D, E), dtype=jnp.float32) * s, 'br': jnp.zeros((E,), dtype=jnp.float32)}
    _L0_ffn_all = _L0_ffn_setup()
    _L0_ffn_in = {k: v for k, v in _L0_ffn_all.items() if k in ('W1', 'b1', 'W2', 'b2', 'Wr', 'br')}
    del _L0_ffn_all
    return {'x': x, 'ctx_1024': ctx_1024, 'g_xattn': g_xattn, 'g_ffn': g_ffn, 'L0_xattn_Wq': _L0_xattn_in['Wq'], 'L0_xattn_bq': _L0_xattn_in['bq'], 'L0_xattn_Wk': _L0_xattn_in['Wk'], 'L0_xattn_bk': _L0_xattn_in['bk'], 'L0_xattn_Wv': _L0_xattn_in['Wv'], 'L0_xattn_bv': _L0_xattn_in['bv'], 'L0_xattn_Wo': _L0_xattn_in['Wo'], 'L0_xattn_bo': _L0_xattn_in['bo'], 'L0_ffn_W1': _L0_ffn_in['W1'], 'L0_ffn_b1': _L0_ffn_in['b1'], 'L0_ffn_W2': _L0_ffn_in['W2'], 'L0_ffn_b2': _L0_ffn_in['b2'], 'L0_ffn_Wr': _L0_ffn_in['Wr'], 'L0_ffn_br': _L0_ffn_in['br']}

def reference(x, ctx_1024, g_xattn, g_ffn, L0_xattn_Wq, L0_xattn_bq, L0_xattn_Wk, L0_xattn_bk, L0_xattn_Wv, L0_xattn_bv, L0_xattn_Wo, L0_xattn_bo, L0_ffn_W1, L0_ffn_b1, L0_ffn_W2, L0_ffn_b2, L0_ffn_Wr, L0_ffn_br):
    import jax
    import jax.numpy as jnp

    def _L0_xattn_ref(query, key, value, Wq, bq, Wk, bk, Wv, bv, Wo, bo):
        import jax, jax.numpy as jnp
        import numpy as np
        import math
        D_MODEL = 128
        NHEAD = 16
        FACTOR = 1
        B, L = (2, 512)

        def _autocorr_forward(query, key, value, Wq, bq, Wk, bk, Wv, bv, Wo, bo):
            Bq, Lq, d = query.shape
            Lk = key.shape[1]
            H = NHEAD
            Dk = d // H
            Q = (query @ Wq + bq).reshape(Bq, Lq, H, Dk).transpose(0, 2, 1, 3)
            K = (key @ Wk + bk).reshape(Bq, Lk, H, Dk).transpose(0, 2, 1, 3)
            V = (value @ Wv + bv).reshape(Bq, Lk, H, Dk).transpose(0, 2, 1, 3)
            if Lk > Lq:
                K = K[:, :, :Lq, :]
                V = V[:, :, :Lq, :]
            elif Lq > Lk:
                pad = [(0, 0), (0, 0), (0, Lq - Lk), (0, 0)]
                K = jnp.pad(K, pad)
                V = jnp.pad(V, pad)
            Lloc = Lq
            Qf = jnp.fft.rfft(Q, axis=2)
            Kf = jnp.fft.rfft(K, axis=2)
            corr = jnp.fft.irfft(Qf * jnp.conj(Kf), n=Lloc, axis=2)
            corr_mean = corr.mean(axis=-1)
            top_k = min(max(1, int(FACTOR * math.log(Lloc + 1))), Lloc)
            w, idx = jax.lax.top_k(corr_mean, top_k)
            w = jax.nn.softmax(w, axis=-1)
            ar = jnp.arange(Lloc)
            shifted = (ar[None, None, None, :] + idx[..., None]) % Lloc
            rolled = jnp.take_along_axis(V[:, :, None, :, :], shifted[..., None], axis=3)
            out = jnp.einsum('bhk,bhkld->bhld', w, rolled)
            out = out.transpose(0, 2, 1, 3).reshape(Bq, Lq, d)
            return out @ Wo + bo
        return _autocorr_forward(query, key, value, Wq, bq, Wk, bk, Wv, bv, Wo, bo)

    def _L0_ffn_ref(x, W1, b1, W2, b2, Wr, br):
        import jax, jax.numpy as jnp
        import numpy as np
        from jax import lax
        D = 128
        H = 512
        E = 8
        TOPK = 2
        B, S, _ = x.shape
        xf = x.reshape(-1, D)
        logits = xf @ Wr + br
        topv, _ = lax.top_k(logits, TOPK)
        thresh = topv[:, TOPK - 1:TOPK]
        masked = jnp.where(logits >= thresh, logits, -jnp.inf)
        weights = jax.nn.softmax(masked, axis=-1)
        h = jax.nn.gelu(jnp.einsum('td,edh->eth', xf, W1) + b1[:, None, :], approximate=False)
        expert_out = jnp.einsum('eth,ehd->etd', h, W2) + b2[:, None, :]
        out = jnp.einsum('etd,te->td', expert_out, weights)
        return out.reshape(B, S, D)
    x = x + jnp.tanh(g_xattn[0]) * _L0_xattn_ref(_layernorm(x, axis=-1), ctx_1024, ctx_1024, L0_xattn_Wq, L0_xattn_bq, L0_xattn_Wk, L0_xattn_bk, L0_xattn_Wv, L0_xattn_bv, L0_xattn_Wo, L0_xattn_bo)
    x = x + jnp.tanh(g_ffn[0]) * _L0_ffn_ref(_layernorm(x, axis=-1), L0_ffn_W1, L0_ffn_b1, L0_ffn_W2, L0_ffn_b2, L0_ffn_Wr, L0_ffn_br)
    return x

_drawn_inputs = setup_inputs


def setup_inputs(seed=0):
    import zlib

    import numpy as np

    out = dict(_drawn_inputs(seed))
    spreads = {'L0_xattn_bq': (0.0, 2.0),
     'L0_xattn_bk': (0.0, 2.0),
     'L0_xattn_bv': (0.0, 0.413),
     'L0_xattn_bo': (0.0, 0.1),
     'L0_ffn_b1': (0.0, 0.498),
     'L0_ffn_b2': (0.0, 0.1),
     'L0_ffn_br': (0.0, 0.1)}
    factors = {'L0_xattn_Wq': 8.416, 'L0_xattn_Wk': 8.621}
    for name, (base, spread) in spreads.items():
        noise = np.random.default_rng([zlib.crc32(name.encode()), seed]).standard_normal(out[name].shape)
        drawn = base * np.exp(spread * noise) if base else spread * noise
        out[name] = jnp.asarray(drawn.astype(out[name].dtype))
    for name, factor in factors.items():
        out[name] = (out[name] * factor).astype(out[name].dtype)
    return out
```

```python
from contextlib import ExitStack

import numpy as np

import concourse.bass as bass
from concourse import mybir

F32 = mybir.dt.float32
F32R = mybir.dt.float32r
U32 = mybir.dt.uint32
I32 = mybir.dt.int32
ALU = mybir.AluOpType
ACT = mybir.ActivationFunctionType
AX = mybir.AxisListType

B, L, D = 16, 56, 128
NH = 16
DK = D // NH
TOP = 4
E, H = 8, 512
ROUTES = 3
HC = H // D
RING = 2
NT = B // 2
PT = 2 * L
NF = L // 2 + 1
SP = 2 * NF
PS = 2 * SP
HT = NT // 2
HS = HT * PS
TOK = HT * PT
EPS = 1e-5
RSQRT_MAGIC = 0x5F3759DF

C_FWD = 0
C_ID = C_FWD + PS
TAB_A = C_ID + D
C_SUM = 0
C_INV = C_SUM + NH
C_MASK = C_INV + 2 * L
C_FWD1 = C_MASK + 2 * NH
C_IOTA = C_FWD1 + SP
C_OUT = C_IOTA + L
TAB_B = C_OUT + PT


def tables():
    pos, freq = np.arange(L), np.arange(NF)
    angle = 2 * np.pi * ((pos[:, None] * freq[None, :]) % L) / L
    cos, sin = np.cos(angle), np.sin(angle)
    fwd = np.concatenate([cos, sin], 1)
    both = np.where((freq == 0) | (freq == L // 2), 1.0, 2.0)[:, None]
    a, b = np.zeros((D, TAB_A)), np.zeros((D, TAB_B))
    a[:L, C_FWD:C_FWD + SP] = fwd
    a[L:PT, C_FWD + SP:C_FWD + PS] = fwd
    a[:, C_ID:C_ID + D] = np.eye(D)
    b[:, C_SUM:C_SUM + NH] = np.arange(D)[:, None] // DK == np.arange(NH)
    scale = 1.0 / (L * DK)
    same = np.concatenate([both * cos.T, both * cos.T]) * scale
    cross = np.concatenate([-both * sin.T, both * sin.T]) * scale
    back = np.concatenate([both * cos.T, both * sin.T]) / L
    for n in range(2):
        rows = slice(n * SP, (n + 1) * SP)
        b[rows, C_INV:C_INV + L] = same
        b[rows, C_INV + L:C_INV + 2 * L] = cross
        b[rows, C_MASK + n * NH:C_MASK + (n + 1) * NH] = 1.0
        b[rows, C_OUT + n * L:C_OUT + (n + 1) * L] = back
    b[:L, C_FWD1:C_FWD1 + SP] = fwd
    b[:, C_IOTA:C_IOTA + L] = pos
    return a.astype(np.float32), b.astype(np.float32)


def build(nc, x, ctx_in, g_xattn, g_ffn, wq, bq, wk, bk, wv, bv, wo, bo, w1, b1, w2, b2, wr, br,
          tab_a, tab_b, out, route_dram):
    with ExitStack() as stack:
        def sb(name, shape, dt=F32):
            return stack.enter_context(nc.sbuf_tensor(name, shape, dt))

        def sem(name):
            return stack.enter_context(nc.semaphore(name))

        ta = sb("ta", [D, TAB_A])
        tb = sb("tb", [D, TAB_B])
        x_sb = sb("x_sb", [PT, NT, D])
        c_sb = sb("c_sb", [PT, NT, D])
        wq_sb, wk_sb, wv_sb, wo_sb = (sb(n, [D, D]) for n in ("wq_sb", "wk_sb", "wv_sb", "wo_sb"))
        wr_sb = sb("wr_sb", [D, E])
        br_sb = sb("br_sb", [PT, E])
        bo_sb = sb("bo_sb", [PT, D])
        g_sb = sb("g_sb", [D, 2])
        NB = 3 + E + E * HC
        brow = sb("brow", [NB, D])
        w1_sb = sb("w1_sb", [D, RING, H])
        w2_sb = sb("w2_sb", [D, RING, HC, D])
        tanh_g = sb("tanh_g", [D, 2])
        bcol = sb("bcol", [D, NB])
        b56 = sb("b56", [D, 3])
        xres = sb("xres", [PT, NT, D])
        stat = sb("stat", [PT, NT, 6])
        msum = sb("msum", [PT, NT])
        mdif = sb("mdif", [PT, NT])
        vsum = sb("vsum", [PT, NT])
        mean = sb("mean", [PT, NT])
        var = sb("var", [PT, NT])
        nhv = sb("nhv", [PT, NT])
        guess = sb("guess", [PT, NT], I32)
        rs_a = sb("rs_a", [PT, NT])
        rs_b = sb("rs_b", [PT, NT])
        rstd = sb("rstd", [PT, NT])
        xn = sb("xn", [PT, NT, D])
        cf = sb("cf", [D, 2, HS])
        xf = sb("xf", [D, 2, HS])
        qf = sb("qf", [D, 2, HS])
        kf = sb("kf", [D, 2, HS])
        vf = sb("vf", [D, 2, HS])
        prod = sb("prod", [D, 2, 2, HS])
        rsb = sb("rsb", [PS, 2, NT, 2 * NH])
        top8 = sb("top8", [D, 2, 8])
        idx8 = sb("idx8", [D, 2, 8], U32)
        idxf = sb("idxf", [D, 2, TOP])
        dif4 = sb("dif4", [D, 2, TOP])
        exp4 = sb("exp4", [D, 2, TOP])
        sum4 = sb("sum4", [D, 2])
        inv4 = sb("inv4", [D, 2])
        wgt4 = sb("wgt4", [D, 2, TOP])
        picks = sb("picks", [D, 2, TOP, L])
        wtau = sb("wtau", [D, 2, L])
        wexp = sb("wexp", [L, B, NH, DK])
        t1 = sb("t1", [D, 2, HS])
        t2 = sb("t2", [D, 2, HS])
        of = sb("of", [D, 2, HS])
        y_sb = sb("y_sb", [PS, NT, D])
        x2 = sb("x2", [PT, NT, D])
        logit = sb("logit", [PT, NT, E])
        ltop = sb("ltop", [PT, NT, 8])
        ldif = sb("ldif", [PT, NT, E])
        lexp = sb("lexp", [PT, NT, E])
        lmask = sb("lmask", [PT, NT, E])
        lsum = sb("lsum", [PT, NT])
        linv = sb("linv", [PT, NT])
        route = sb("route", [PT, NT, E])
        route_t = sb("route_t", [E, 2, TOK])
        route_b = sb("route_b", [D, ROUTES, 2, TOK])
        xt = sb("xt", [D, 2, TOK])
        xth = sb("xth", [D, 2, TOK], F32R)
        xtl = sb("xtl", [D, 2, TOK], F32R)
        w1h = sb("w1h", [D, E, H], F32R)
        w1l = sb("w1l", [D, E, H], F32R)
        w2h = sb("w2h", [D, E, HC, D], F32R)
        w2l = sb("w2l", [D, E, HC, D], F32R)
        hid = prod[:, :, :, :].rearrange("p k a s -> p (k a s)")[:, 0:4 * TOK].rearrange("p (s a t) -> p s a t", s=2, a=2)
        hidh = sb("hidh", [D, 2, 2, TOK], F32R)
        hidl = sb("hidl", [D, 2, 2, TOK], F32R)
        scaled = kf[:, :, 0:TOK]
        acc = qf[:, :, 0:TOK]
        o_sb = sb("o_sb", [PT, NT, D])

        bank = stack.enter_context(nc.psum_tensor("bank", [D, 8, 512], F32))
        ident = ta[:, C_ID:C_ID + D]

        in_ta, in_tb, in_c, in_x = sem("in_ta"), sem("in_tb"), sem("in_c"), sem("in_x")
        in_wq, in_wk, in_wv, in_wo = sem("in_wq"), sem("in_wk"), sem("in_wv"), sem("in_wo")
        in_brow, in_small, in_wr = sem("in_brow"), sem("in_small"), sem("in_wr")
        in_w1 = [sem(f"in_w1_{e}") for e in range(E)]
        in_w2 = [sem(f"in_w2_{e}") for e in range(E)]
        dve, actc = sem("dve_done"), sem("act_done")
        bias_t, bias_ok = sem("bias_transposed"), sem("bias_columns_ready")
        c_spec, cf_ok = sem("context_spectra"), sem("context_spectra_in_sbuf")
        xn_ok, x_spec, xf_ok = sem("xn_ready"), sem("x_spectra"), sem("x_spectra_in_sbuf")
        k_proj, v_proj, q_proj = sem("k_projected"), sem("v_projected"), sem("q_projected")
        k_ok, v_ok, q_ok = sem("k_in_sbuf"), sem("v_in_sbuf"), sem("q_in_sbuf")
        prod_ok, heads, rsb_ok = sem("products_ready"), sem("head_sums"), sem("head_sums_in_sbuf")
        corr, dif_ok, exp_ok = sem("correlations"), sem("top_differences"), sem("top_exponentials")
        wtau_ok, wtau_t, wexp_ok = sem("shift_weights"), sem("shift_weights_transposed"), sem("shift_weights_repeated")
        wspec, of_ok = sem("weight_spectra"), sem("output_spectra")
        y_mm, y_ok, attn = sem("y_products"), sem("y_in_sbuf"), sem("attention_out")
        tanh_ok, xres_ok = sem("gates_ready"), sem("residual_with_bias")
        x2n_ok, xt_mm, xt_ok = sem("x2_normalised"), sem("x2_transposed"), sem("x2_split")
        xtf_ok = sem("x2_transposed_in_sbuf")
        logit_mm, ldif_ok, lexp_ok = sem("logits"), sem("logit_differences"), sem("logit_exponentials")
        route_ok, route_mm, route_sb, route_out = sem("routes"), sem("routes_transposed"), sem("routes_in_sbuf"), sem("routes_in_dram")
        in_route = [sem(f"route_weights_{e}") for e in range(E)]
        w1_split, w2_split, pool = sem("w1_split"), sem("w2_split"), sem("pool_done")
        h_mm, gelu_ok, hid_hi, hid_ok = sem("hidden_products"), sem("gelu_done"), sem("hidden_lead"), sem("hidden_split")
        y_expert, scaled_ok = sem("expert_products"), sem("expert_taken")
        acc_ok, back_mm, o_ok, stored = sem("experts_summed"), sem("sum_transposed"), sem("result_ready"), sem("stored")

        def spectra(t, half):
            return t[:, half, :].rearrange("p (b s f) -> p b s f", s=2, f=NF)

        block = stack.enter_context(nc.Block())

        @block.sync
        def _(sp):
            for n in range(2):
                sp.dma_start(c_sb[n * L:(n + 1) * L, :, :],
                             ctx_in.rearrange("(i n) l d -> n l i d", n=2)[n, 0:L]).then_inc(in_c, 16)
            sp.dma_start(x_sb[:, :, :],
                         x.rearrange("b l d -> (b l) d").rearrange("(i p) d -> p i d", p=PT)).then_inc(in_x, 16)
            sp.dma_start(wq_sb[:, :], wq).then_inc(in_wq, 16)
            sp.dma_start(tb[:, :], tab_b).then_inc(in_tb, 16)
            sp.dma_start(wo_sb[:, :], wo).then_inc(in_wo, 16)
            for e in range(E):
                if e >= RING:
                    sp.wait_ge(w1_split, e - RING + 1)
                sp.dma_start(w1_sb[:, e % RING, :], w1[e]).then_inc(in_w1[e], 16)
                if e >= RING:
                    sp.wait_ge(w2_split, e - RING + 1)
                sp.dma_start(w2_sb[:, e % RING, :, :], w2[e].rearrange("(c p) d -> p c d", p=D)).then_inc(in_w2[e], 16)
            for half in range(2):
                sp.wait_ge(route_sb, half + 1)
                sp.dma_start(route_dram[:, half, :], route_t[:, half, :]).then_inc(route_out, 16)
            sp.wait_ge(route_out, 32)
            for e in range(E):
                if e >= ROUTES:
                    sp.wait_ge(scaled_ok, 2 * (e - ROUTES + 1))
                sp.dma_start(route_b[:, e % ROUTES, :, :], route_dram[e:e + 1].broadcast_to([D, 2, TOK])).then_inc(in_route[e], 16)
            for half in range(2):
                sp.wait_ge(o_ok, half + 1)
                sp.dma_start(out.rearrange("b l d -> (b l) d").rearrange("(i p) d -> p i d", p=PT)[:, half * HT:(half + 1) * HT],
                             o_sb[:, half * HT:(half + 1) * HT, :]).then_inc(stored, 16)
            sp.wait_ge(stored, 32)

        @block.gpsimd
        def _(gp):
            gp.wait_ge(in_x, 16)
            gp.wait_ge(in_small, 64)
            gp.wait_ge(tanh_ok, 1)
            gp.tensor_scalar(bo_sb[:, :], bo_sb[:, :], tanh_g[0:PT, 0:1], None, ALU.mult).then_inc(pool, 1)
            gp.wait_ge(pool, 1)
            gp.tensor_tensor(xres[:, :, :], x_sb[:, :, :], bo_sb[:, :].unsqueeze(1).broadcast_to([PT, NT, D]),
                             ALU.add).then_inc(xres_ok, 1)
            n = 1
            for e in range(E):
                for raw, hi, lo, arrived, split in ((w1_sb[:, e % RING, :], w1h[:, e, :], w1l[:, e, :], in_w1[e], w1_split),
                                                    (w2_sb[:, e % RING, :, :], w2h[:, e, :, :], w2l[:, e, :, :], in_w2[e], w2_split)):
                    gp.wait_ge(arrived, 16)
                    gp.tensor_copy(hi, raw).then_inc(pool, 1)
                    n += 1
                    gp.wait_ge(pool, n)
                    gp.tensor_tensor(lo, raw, hi.bitcast(F32), ALU.subtract).then_inc(split, 1)

        @block.scalar
        def _(act):
            act.dma_start(ta[:, :], tab_a).then_inc(in_ta, 16)
            act.dma_start(wk_sb[:, :], wk).then_inc(in_wk, 16)
            act.dma_start(wv_sb[:, :], wv).then_inc(in_wv, 16)
            for n, row in enumerate((bq, bk, bv)):
                act.dma_start(brow[n:n + 1, :], row.unsqueeze(0)).then_inc(in_brow, 16)
            act.dma_start(brow[3:3 + E, :], b2).then_inc(in_brow, 16)
            act.dma_start(brow[3 + E:NB, :], b1.rearrange("e (c p) -> (e c) p", p=D)).then_inc(in_brow, 16)
            act.dma_start(g_sb[:, 0:1], g_xattn.unsqueeze(0).broadcast_to([D, 1])).then_inc(in_small, 16)
            act.dma_start(g_sb[:, 1:2], g_ffn.unsqueeze(0).broadcast_to([D, 1])).then_inc(in_small, 16)
            act.dma_start(bo_sb[:, :], bo.unsqueeze(0).broadcast_to([PT, D])).then_inc(in_small, 16)
            act.dma_start(br_sb[:, :], br.unsqueeze(0).broadcast_to([PT, E])).then_inc(in_small, 16)
            act.dma_start(wr_sb[:, :], wr).then_inc(in_wr, 16)
            for half in range(2):
                act.wait_ge(c_spec, half + 1)
                act.copy(cf[:, half, :], bank[:, half, 0:HS]).then_inc(cf_ok, 1)
            act.wait_ge(in_small, 64)
            act.activation(tanh_g[:, :], g_sb[:, :], ACT.Tanh).then_inc(tanh_ok, 1)
            act.wait_ge(bias_ok, 1)
            chain = 0
            for spectrum, first, done, col, projected in ((kf, 4, k_ok, 1, k_proj), (vf, 6, v_ok, 2, v_proj)):
                for half in range(2):
                    act.wait_ge(projected, half + 1)
                    act.copy(spectrum[:, half, :], bank[:, first + half, 0:HS]).then_inc(actc, 1)
                    chain += 1
                    act.wait_ge(actc, chain)
                    dc = spectra(spectrum, half)[:, :, 0, 0]
                    act.activation(dc, dc, ACT.Identity, bias=b56[:, col:col + 1]).then_inc(done, 1)
            act.wait_ge(dif_ok, 1)
            act.activation(exp4[:, :, :], dif4[:, :, :], ACT.Exp).then_inc(exp_ok, 1)
            act.wait_ge(wtau_t, 2)
            act.copy(wexp[:, HT * 2:, :, :], bank[0:L, 7, 0:D].rearrange("p (b h) -> p b h", h=NH)
                     .unsqueeze(3).broadcast_to([L, NT, NH, DK])).then_inc(wexp_ok, 1)
            for half in range(2):
                act.wait_ge(y_mm, half + 1)
                act.copy(y_sb[:, half * HT:(half + 1) * HT, :],
                         bank[0:PS, half, :].rearrange("p (i d) -> p i d", d=D)).then_inc(y_ok, 1)
            act.wait_ge(ldif_ok, 1)
            act.activation(lexp[:, :, :], ldif[:, :, :], ACT.Exp).then_inc(lexp_ok, 1)
            for n in range(E * HC):
                e, c, slot = n // HC, n % HC, n % 2
                act.wait_ge(h_mm, n + 1)
                if n >= 2:
                    act.wait_ge(hid_ok, n - 1)
                act.activation(hid[:, slot, :, :], bank[:, 2 * slot:2 * slot + 2, 0:TOK], ACT.Gelu,
                               bias=bcol[:, 3 + E + n:4 + E + n]).then_inc(gelu_ok, 1)
                act.wait_ge(gelu_ok, n + 1)
                if n >= 2:
                    act.wait_ge(y_expert, n - 1)
                act.copy(hidh[:, slot, :, :], hid[:, slot, :, :]).then_inc(hid_hi, 1)

        @block.vector
        def _(ve):
            count = [0]

            def link(instruction):
                count[0] += 1
                instruction.then_inc(dve, 1)
                ve.wait_ge(dve, count[0])

            def mark(instruction):
                count[0] += 1
                instruction.then_inc(dve, 1)

            def normalise(src, ready):
                for i in range(NT):
                    mark(ve.bn_stats(stat[:, i, :], src[:, i, :]))
                ve.wait_ge(dve, count[0])
                mark(ve.tensor_tensor(msum[:, :], stat[:, :, 1], stat[:, :, 4], ALU.add))
                mark(ve.tensor_tensor(mdif[:, :], stat[:, :, 1], stat[:, :, 4], ALU.subtract))
                link(ve.tensor_tensor(vsum[:, :], stat[:, :, 2], stat[:, :, 5], ALU.add))
                mark(ve.tensor_scalar(mean[:, :], msum[:, :], 0.5, None, ALU.mult))
                link(ve.tensor_tensor(mdif[:, :], mdif[:, :], mdif[:, :], ALU.mult))
                link(ve.scalar_tensor_tensor(out=var[:, :], in0=mdif[:, :], scalar=D / 4.0, in1=vsum[:, :],
                                             op0=ALU.mult, op1=ALU.add))
                link(ve.tensor_scalar(var[:, :], var[:, :], 1.0 / D, EPS, ALU.mult, ALU.add))
                mark(ve.tensor_scalar(nhv[:, :], var[:, :], -0.5, None, ALU.mult))
                link(ve.tensor_scalar(guess[:, :], var[:, :].bitcast(I32), 1, None, ALU.logical_shift_right))
                link(ve.tensor_scalar(rs_a[:, :].bitcast(I32), guess[:, :], -1.0, float(RSQRT_MAGIC), ALU.mult, ALU.add))
                here, there = rs_a, rstd
                for _ in range(3):
                    link(ve.tensor_tensor(rs_b[:, :], here[:, :], here[:, :], ALU.mult))
                    link(ve.tensor_tensor(rs_b[:, :], rs_b[:, :], nhv[:, :], ALU.mult))
                    link(ve.scalar_tensor_tensor(out=there[:, :], in0=rs_b[:, :], scalar=1.5, in1=here[:, :],
                                                 op0=ALU.add, op1=ALU.mult))
                    here, there = there, here
                for i in range(NT):
                    ve.tensor_scalar(xn[:, i, :], src[:, i, :], mean[:, i:i + 1], here[:, i:i + 1],
                                     ALU.subtract, ALU.mult).then_inc(ready, 1)

            ve.wait_ge(in_x, 16)
            normalise(x_sb, xn_ok)
            ve.wait_ge(bias_t, 1)
            link(ve.tensor_copy(bcol[:, :], bank[:, 7, HS:HS + NB]))
            ve.tensor_scalar(b56[:, :], bcol[:, 0:3], float(L), None, ALU.mult).then_inc(bias_ok, 1)
            for half in range(2):
                ve.wait_ge(x_spec, half + 1)
                ve.tensor_copy(xf[:, half, :], bank[:, 2 + half, 0:HS]).then_inc(xf_ok, 1)
            ve.wait_ge(bias_ok, 1)
            for half in range(2):
                ve.wait_ge(q_proj, half + 1)
                link(ve.tensor_copy(qf[:, half, :], bank[:, half, 0:HS]))
                dc = spectra(qf, half)[:, :, 0, 0]
                link(ve.tensor_scalar(dc, dc, b56[:, 0:1], None, ALU.add))
                ve.wait_ge(k_ok, half + 1)
                ve.tensor_tensor(prod[:, 0, half, :], qf[:, half, :], kf[:, half, :], ALU.mult).then_inc(prod_ok, 1)
                p2, q2, k2 = (spectra(t, half) for t in (prod[:, 1], qf, kf))
                for s in range(2):
                    ve.tensor_tensor(p2[:, :, s, :], q2[:, :, s, :], k2[:, :, 1 - s, :], ALU.mult).then_inc(prod_ok, 1)
            for half in range(2):
                ve.wait_ge(heads, half + 1)
                for kind in range(2):
                    src = bank[0:PS, 2 + half, 0:2 * HT * NH].rearrange("p (k i h) -> p k i h", k=2, h=NH)[:, kind]
                    ve.tensor_tensor(rsb[:, kind, half * HT:(half + 1) * HT, :].rearrange("p i (n h) -> p i n h", n=2),
                                     src.unsqueeze(2).broadcast_to([PS, HT, 2, NH]),
                                     tb[0:PS, C_MASK:C_MASK + 2 * NH].rearrange("p (n h) -> p n h", n=2)
                                     .unsqueeze(1).broadcast_to([PS, HT, 2, NH]), ALU.mult).then_inc(rsb_ok, 1)
            ve.wait_ge(corr, 2)
            cps = bank[:, 4:6, 0:L]
            for t in range(2):
                mark(ve.max(top8[:, t, :], cps[:, t, :]))
            ve.wait_ge(dve, count[0])
            ve.tensor_tensor(dif4[:, :, :], top8[:, :, 0:TOP], top8[:, :, 0:1].broadcast_to([D, 2, TOP]),
                             ALU.subtract).then_inc(dif_ok, 1)
            for t in range(2):
                mark(ve.max_index(idx8[:, t, :], top8[:, t, :], cps[:, t, :]))
            ve.wait_ge(dve, count[0])
            link(ve.tensor_copy(idxf[:, :, :], idx8[:, :, 0:TOP]))
            ve.wait_ge(exp_ok, 1)
            link(ve.tensor_reduce(sum4[:, :], exp4[:, :, :], AX.X, ALU.add))
            link(ve.reciprocal(inv4[:, :], sum4[:, :]))
            link(ve.tensor_tensor(wgt4[:, :, :], exp4[:, :, :], inv4[:, :].unsqueeze(2).broadcast_to([D, 2, TOP]), ALU.mult))
            for t in range(2):
                for k in range(TOP):
                    mark(ve.tensor_scalar(picks[:, t, k, :], tb[:, C_IOTA:C_IOTA + L], idxf[:, t, k:k + 1],
                                          wgt4[:, t, k:k + 1], ALU.is_equal, ALU.mult))
                ve.wait_ge(dve, count[0])
                ve.tensor_reduce(wtau[:, t, :], picks[:, t, :, :].rearrange("p k l -> p l k"), AX.X, ALU.add).then_inc(wtau_ok, 1)
            ve.wait_ge(wtau_t, 1)
            ve.tensor_copy(wexp[:, 0:NT, :, :], bank[0:L, 6, 0:D].rearrange("p (b h) -> p b h", h=NH)
                           .unsqueeze(3).broadcast_to([L, NT, NH, DK])).then_inc(wexp_ok, 1)
            ve.wait_ge(v_ok, 2)
            for half in range(2):
                ve.wait_ge(wspec, half + 1)
                ws = bank[:, 2 + half, 0:HS]
                wsv, v2, t1v, t2v, ov = (spectra(t, half) if t is not bank else
                                         ws.rearrange("p (b s f) -> p b s f", s=2, f=NF) for t in (bank, vf, t1, t2, of))
                mark(ve.tensor_tensor(t1[:, half, :], ws, vf[:, half, :], ALU.mult))
                for s in range(2):
                    mark(ve.tensor_tensor(t2v[:, :, s, :], wsv[:, :, s, :], v2[:, :, 1 - s, :], ALU.mult))
                ve.wait_ge(dve, count[0])
                ve.tensor_tensor(ov[:, :, 0, :], t1v[:, :, 0, :], t1v[:, :, 1, :], ALU.add).then_inc(of_ok, 1)
                ve.tensor_tensor(ov[:, :, 1, :], t2v[:, :, 0, :], t2v[:, :, 1, :], ALU.subtract).then_inc(of_ok, 1)
            ve.wait_ge(xres_ok, 1)
            ve.wait_ge(tanh_ok, 1)
            for half in range(2):
                tiles = slice(half * HT, (half + 1) * HT)
                ve.wait_ge(attn, half + 1)
                mark(ve.scalar_tensor_tensor(out=x2[:, tiles, :], in0=bank[0:PT, 4 + half, :].rearrange("p (i d) -> p i d", d=D),
                                             scalar=tanh_g[0:PT, 0:1], in1=xres[:, tiles, :], op0=ALU.mult, op1=ALU.add))
            ve.wait_ge(dve, count[0])
            ve.wait_ge(x_spec, 2)
            normalise(x2, x2n_ok)
            for half in range(2):
                ve.wait_ge(xt_mm, half + 1)
                ve.tensor_copy(xt[:, half, :], bank[:, 6 + half, 0:TOK]).then_inc(xtf_ok, 1)
            for half in range(2):
                ve.wait_ge(xtf_ok, half + 1)
                link(ve.tensor_copy(xth[:, half, :], xt[:, half, :]))
                ve.tensor_tensor(xtl[:, half, :], xt[:, half, :], xth[:, half, :].bitcast(F32), ALU.subtract).then_inc(xt_ok, 1)
            ve.wait_ge(in_small, 64)
            ve.wait_ge(logit_mm, 1)
            link(ve.tensor_tensor(logit[:, :, :], bank[0:PT, 4, 0:NT * E].rearrange("p (i e) -> p i e", e=E),
                                  br_sb[:, :].unsqueeze(1).broadcast_to([PT, NT, E]), ALU.add))
            for i in range(NT):
                mark(ve.max(ltop[:, i, :], logit[:, i, :]))
            ve.wait_ge(dve, count[0])
            ve.tensor_tensor(ldif[:, :, :], logit[:, :, :], ltop[:, :, 0:1].broadcast_to([PT, NT, E]),
                             ALU.subtract).then_inc(ldif_ok, 1)
            mark(ve.tensor_tensor(lmask[:, :, :], logit[:, :, :], ltop[:, :, 1:2].broadcast_to([PT, NT, E]), ALU.is_ge))
            ve.wait_ge(dve, count[0])
            ve.wait_ge(lexp_ok, 1)
            link(ve.tensor_tensor(lexp[:, :, :], lexp[:, :, :], lmask[:, :, :], ALU.mult))
            link(ve.tensor_reduce(lsum[:, :], lexp[:, :, :], AX.X, ALU.add))
            link(ve.reciprocal(linv[:, :], lsum[:, :]))
            ve.tensor_tensor(route[:, :, :], lexp[:, :, :], linv[:, :].unsqueeze(2).broadcast_to([PT, NT, E]),
                             ALU.mult).then_inc(route_ok, 1)

            def take_routes():
                for half in range(2):
                    ve.wait_ge(route_mm, half + 1)
                    ve.tensor_copy(route_t[:, half, :], bank[0:E, 4 + half, 0:TOK]).then_inc(route_sb, 1)

            def take_expert(e):
                ve.wait_ge(y_expert, HC * (e + 1))
                ve.wait_ge(in_route[e], 16)
                for half in range(2):
                    o_ps = bank[:, 6 - 2 * (e % 2) + half, 0:TOK]
                    into = acc if e == 0 else scaled
                    done = ve.scalar_tensor_tensor(out=into[:, half, :], in0=o_ps, scalar=bcol[:, 3 + e:4 + e],
                                                   in1=route_b[:, e % ROUTES, half, :], op0=ALU.add, op1=ALU.mult)
                    done.then_inc(scaled_ok, 1)
                    if e:
                        ve.wait_ge(scaled_ok, 2 * e + half + 1)
                        done = ve.tensor_tensor(acc[:, half, :], acc[:, half, :], scaled[:, half, :], ALU.add)
                        done.then_inc(acc_ok, 1)

            for n in range(E * HC):
                slot = n % 2
                ve.wait_ge(hid_hi, n + 1)
                if n >= 2:
                    ve.wait_ge(y_expert, n - 1)
                ve.tensor_tensor(hidl[:, slot, :, :], hid[:, slot, :, :], hidh[:, slot, :, :].bitcast(F32),
                                 ALU.subtract).then_inc(hid_ok, 1)
                if n == 0:
                    take_routes()
                if n % HC == 1 and n > HC:
                    take_expert(n // HC - 1)
            take_expert(E - 1)
            for half in range(2):
                tiles = slice(half * HT, (half + 1) * HT)
                ve.wait_ge(back_mm, half + 1)
                ve.scalar_tensor_tensor(out=o_sb[:, tiles, :], in0=bank[0:PT, half, :].rearrange("p (i d) -> p i d", d=D),
                                        scalar=tanh_g[0:PT, 1:2], in1=x2[:, tiles, :], op0=ALU.mult, op1=ALU.add).then_inc(o_ok, 1)

        @block.tensor
        def _(pe):
            pe.wait_ge(in_ta, 16)
            pe.wait_ge(in_brow, 80)
            pe.transpose(bank[:, 7, HS:HS + NB], brow[:, :], ident[0:NB, 0:NB]).then_inc(bias_t, 1)

            def to_spectra(src, first, i):
                return pe.matmul(bank[:, first + i // HT, (i % HT) * PS:(i % HT + 1) * PS], src[:, i, :],
                                 ta[0:PT, C_FWD:C_FWD + PS], start=(i % HT == 0), stop=(i % HT == HT - 1),
                                 skip_group_check=True)

            pe.wait_ge(in_c, 32)
            for i in range(NT):
                mm = to_spectra(c_sb, 0, i)
                if i % HT == HT - 1:
                    mm.then_inc(c_spec, 1)
            for weight, arrived, first, projected in ((wk_sb, in_wk, 4, k_proj), (wv_sb, in_wv, 6, v_proj)):
                pe.wait_ge(arrived, 16)
                if weight is wv_sb:
                    pe.wait_ge(bias_ok, 1)
                for half in range(2):
                    pe.wait_ge(cf_ok, half + 1)
                    pe.matmul(bank[:, first + half, 0:HS], weight[:, :], cf[:, half, :], start=True, stop=True).then_inc(projected, 1)
            for i in range(NT):
                pe.wait_ge(xn_ok, i + 1)
                mm = to_spectra(xn, 2, i)
                if i % HT == HT - 1:
                    mm.then_inc(x_spec, 1)
            pe.wait_ge(in_wq, 16)
            for half in range(2):
                pe.wait_ge(xf_ok, half + 1)
                pe.matmul(bank[:, half, 0:HS], wq_sb[:, :], xf[:, half, :], start=True, stop=True).then_inc(q_proj, 1)
            pe.wait_ge(in_tb, 16)
            for half in range(2):
                for kind in range(2):
                    pe.wait_ge(prod_ok, 3 * half + 1 + 2 * kind)
                    for i in range(HT):
                        at = (kind * HT + i) * NH
                        mm = pe.matmul(bank[0:PS, 2 + half, at:at + NH], prod[:, kind, half, i * PS:(i + 1) * PS],
                                       tb[:, C_SUM:C_SUM + NH], start=(kind == 0 and i == 0), stop=True,
                                       skip_group_check=True)
                mm.then_inc(heads, 1)
            for t in range(2):
                pe.wait_ge(rsb_ok, 2 * t + 2)
                for j in range(HT):
                    for kind in range(2):
                        mm = pe.matmul(bank[32 * j:32 * j + 32, 4 + t, 0:L], rsb[:, kind, HT * t + j, :],
                                       tb[0:PS, C_INV + kind * L:C_INV + (kind + 1) * L],
                                       start=(kind == 0), stop=(kind == 1), skip_group_check=True,
                                       tile_position=(0, 32 * j))
                mm.then_inc(corr, 1)
            pe.wait_ge(v_ok, 2)
            for t in range(2):
                pe.wait_ge(wtau_ok, t + 1)
                pe.transpose(bank[0:L, 6 + t, 0:D], wtau[:, t, :], ident).then_inc(wtau_t, 1)
            pe.wait_ge(wexp_ok, 2)
            pe.wait_ge(rsb_ok, 4)
            for b in range(B):
                half, i = b // NT, b % NT
                mm = pe.matmul(bank[:, 2 + half, i * SP:(i + 1) * SP], wexp[:, b, :, :].rearrange("p h r -> p (h r)"),
                               tb[0:L, C_FWD1:C_FWD1 + SP], start=(i == 0), stop=(i == NT - 1), skip_group_check=True)
                if i == NT - 1:
                    mm.then_inc(wspec, 1)
            pe.wait_ge(in_wo, 16)
            for half in range(2):
                pe.wait_ge(of_ok, 2 * half + 2)
                for i in range(HT):
                    mm = pe.matmul(bank[0:PS, half, i * D:(i + 1) * D], of[:, half, i * PS:(i + 1) * PS], wo_sb[:, :],
                                   start=(i == 0), stop=(i == HT - 1), skip_group_check=True)
                mm.then_inc(y_mm, 1)
            for half in range(2):
                pe.wait_ge(y_ok, half + 1)
                pe.matmul(bank[0:PT, 4 + half, :], tb[0:PS, C_OUT:C_OUT + PT],
                          y_sb[:, half * HT:(half + 1) * HT, :].rearrange("p i d -> p (i d)"), start=True, stop=True).then_inc(attn, 1)
            for i in range(NT):
                pe.wait_ge(x2n_ok, i + 1)
                mm = pe.transpose(bank[:, 6 + i // HT, (i % HT) * PT:(i % HT + 1) * PT], xn[:, i, :], ident[0:PT, 0:PT])
                if i % HT == HT - 1:
                    mm.then_inc(xt_mm, 1)
            pe.wait_ge(in_wr, 16)
            for i in range(NT):
                half = i // HT
                pe.wait_ge(xtf_ok, half + 1)
                mm = pe.matmul(bank[0:PT, 4, i * E:(i + 1) * E], xt[:, half, (i % HT) * PT:(i % HT + 1) * PT], wr_sb[:, :],
                               start=(i == 0), stop=(i == NT - 1), skip_group_check=True)
            mm.then_inc(logit_mm, 1)

            def hidden(n):
                e, c, slot = n // HC, n % HC, n % 2
                if c == 0:
                    pe.wait_ge(w1_split, e + 1)
                if n >= 2:
                    pe.wait_ge(gelu_ok, n - 1)
                cols = slice(c * D, (c + 1) * D)
                for k, (w, t) in enumerate(((w1h, xth), (w1h, xtl), (w1l, xth))):
                    for half in range(2):
                        if n == 0:
                            pe.wait_ge(xt_ok, half + 1)
                        mm = pe.matmul(bank[:, 2 * slot + half, 0:TOK], w[:, e, cols], t[:, half, :],
                                       start=(k == 0), stop=(k == 2))
                mm.then_inc(h_mm, 1)

            def routes():
                for i in range(NT):
                    pe.wait_ge(route_ok, 1)
                    at = (i % HT) * PT
                    mm = pe.transpose(bank[0:E, 4 + i // HT, at:at + PT], route[:, i, :], ident[0:PT, 0:PT])
                    if i % HT == HT - 1:
                        mm.then_inc(route_mm, 1)

            def project(n):
                e, c, slot = n // HC, n % HC, n % 2
                if c == 0:
                    pe.wait_ge(w2_split, e + 1)
                    if e == 1:
                        pe.wait_ge(route_sb, 2)
                    if e >= 2:
                        pe.wait_ge(scaled_ok, 2 * (e - 1))
                for k, (w, t) in enumerate(((w2h, hidh), (w2l, hidh), (w2h, hidl))):
                    pe.wait_ge(hid_ok if k == 2 else hid_hi, n + 1)
                    for half in range(2):
                        mm = pe.matmul(bank[:, 6 - 2 * (e % 2) + half, 0:TOK], w[:, e, c, :], t[:, slot, half, :],
                                       start=(c == 0 and k == 0), stop=(c == HC - 1 and k == 2))
                mm.then_inc(y_expert, 1)

            hidden(0)
            for n in range(E * HC):
                if n + 1 < E * HC:
                    hidden(n + 1)
                if n == 0:
                    routes()
                project(n)
            for i in range(NT):
                half = i // HT
                pe.wait_ge(acc_ok, 2 * (E - 2) + half + 1)
                mm = pe.transpose(bank[0:PT, half, (i % HT) * D:(i % HT + 1) * D], acc[:, half, (i % HT) * PT:(i % HT + 1) * PT], ident)
                if i % HT == HT - 1:
                    mm.then_inc(back_mm, 1)


_INS = ["x", "ctx_1024", "g_xattn", "g_ffn"] + ["L0_xattn_" + n for n in ("Wq", "bq", "Wk", "bk", "Wv", "bv", "Wo", "bo")] \
    + ["L0_ffn_" + n for n in ("W1", "b1", "W2", "b2", "Wr", "br")]


def kernel(**inputs):
    import numpy as _np
    import concourse.bacc as _bacc
    from concourse import mybir as _mybir
    from concourse.bass_utils import run_bass_kernel_spmd as _run

    nc = _bacc.Bacc("TRN2", target_bir_lowering=False, num_devices=1)
    tab_a, tab_b = tables()
    arrays, args = {}, []
    for name, a in [(n, inputs[n]) for n in _INS] + [("tab_a", tab_a), ("tab_b", tab_b)]:
        a = _np.ascontiguousarray(a)
        arrays[f"in_{name}"] = a
        args.append(nc.dram_tensor(f"in_{name}", a.shape, _mybir.dt.from_np(a.dtype), kind="ExternalInput").ap())
    out = nc.dram_tensor("out_0", (B, L, D), _mybir.dt.float32, kind="ExternalOutput").ap()
    route = nc.dram_tensor("route_scratch", (E, 2, TOK), _mybir.dt.float32, kind="Internal").ap()
    build(nc, *args, out, route)
    return _run(nc, [arrays], core_ids=[0]).results[0]["out_0"]
```

```python
from contextlib import ExitStack

import numpy as np

import concourse.bass as bass
from concourse import mybir

F32 = mybir.dt.float32
F32R = mybir.dt.float32r
BF16 = mybir.dt.bfloat16
I32 = mybir.dt.int32
ALU = mybir.AluOpType
ACT = mybir.ActivationFunctionType
AX = mybir.AxisListType

B, L, D = 16, 56, 128
NH = 16
DK = D // NH
TOP = 4
LF = L + 8 - TOP
FILL, TAKEN = 3.0e38, -3.0e38
E, H = 8, 512
ROUTES = 3
HC = H // D
RING = 2
WARM = 10
SLOTS = 3
NT = B // 2
PT = 2 * L
NF = L // 2 + 1
SP = 2 * NF
PS = 2 * SP
HT = NT // 2
HS = HT * PS
TOK = HT * PT
EPS = 1e-5
GUESS = float(0x5F1FFFF9)
STEP_A, STEP_B = 0.703952253, 0.703952253 * 2.38924456

A_FWD = 0
A_DC = A_FWD + PS
TAB_A = A_DC + NT
B_SUM = 0
B_INV = B_SUM + NH
B_MASK = B_INV + 2 * L
B_FWD1 = B_MASK + 2 * NH
B_IOTA = B_FWD1 + SP
B_OUT = B_IOTA + L
B_ID = B_OUT + PT
B_REP = B_ID + D
B_OWN = B_REP + D
TAB_B = B_OWN + NT
P_B2, P_B1, P_WR = 0, E, E + E * HC
PCOLS = P_WR + E


def tables():
    pos, freq, part = np.arange(L), np.arange(NF), np.arange(D)
    angle = 2 * np.pi * ((pos[:, None] * freq[None, :]) % L) / L
    cos, sin = np.cos(angle), np.sin(angle)
    fwd = np.concatenate([cos, sin], 1)
    both = np.where((freq == 0) | (freq == L // 2), 1.0, 2.0)[:, None]
    a, b = np.zeros((PT, TAB_A)), np.zeros((D, TAB_B))
    a[:L, A_FWD:A_FWD + SP] = fwd
    a[L:PT, A_FWD + SP:A_FWD + PS] = fwd
    a[0, A_DC:] = L
    b[:, B_SUM:B_SUM + NH] = part[:, None] // DK == np.arange(NH)
    scale = 1.0 / (L * DK)
    same = np.concatenate([both * cos.T, both * cos.T]) * scale
    cross = np.concatenate([-both * sin.T, both * sin.T]) * scale
    back = np.concatenate([both * cos.T, both * sin.T]) / L
    for n in range(2):
        rows = slice(n * SP, (n + 1) * SP)
        b[rows, B_INV:B_INV + L] = same
        b[rows, B_INV + L:B_INV + 2 * L] = cross
        b[rows, B_MASK + n * NH:B_MASK + (n + 1) * NH] = 1.0
        b[rows, B_OUT + n * L:B_OUT + (n + 1) * L] = back
    b[:L, B_FWD1:B_FWD1 + SP] = fwd
    b[:, B_IOTA:B_IOTA + L] = pos
    b[:, B_ID:B_ID + D] = np.eye(D)
    b[:, B_REP:B_REP + D] = part[:, None] % NH == part[None, :] // DK
    b[:, B_OWN:B_OWN + NT] = part[:, None] // NH == np.arange(NT)
    return a.astype(np.float32), b.astype(np.float32)


def build(nc, x, ctx, w_attn, bias_rows, gates, shared_rows, cols, w_experts, tab_a, tab_b, out, route_dram):
    with ExitStack() as stack:
        def sb(name, shape, dt=F32):
            return stack.enter_context(nc.sbuf_tensor(name, shape, dt))

        def sem(name):
            return stack.enter_context(nc.semaphore(name))

        ta = sb("ta", [PT, TAB_A])
        tb = sb("tb", [D, TAB_B])
        x_sb = sb("x_sb", [PT, NT, D])
        c_sb = sb("c_sb", [PT, NT, D])
        wa_sb = sb("wa_sb", [D, 4, D])
        rows_sb = sb("rows_sb", [1, 3, D])
        shared = sb("shared", [PT, D + E])
        g_sb = sb("g_sb", [D, 2])
        col_sb = sb("col_sb", [D, PCOLS])
        we_sb = sb("we_sb", [D, RING, 2, H])
        filler = sb("filler", [D, 512], BF16)
        tanh_g = sb("tanh_g", [D, 2])
        xres = sb("xres", [PT, NT, D])
        stat = sb("stat", [PT, NT, 6])
        mv = sb("mv", [PT, NT, 2])
        var = sb("var", [PT, NT])
        rs_a = sb("rs_a", [PT, NT])
        rs_b = sb("rs_b", [PT, NT])
        rs_c = sb("rs_c", [PT, NT])
        rs_d = sb("rs_d", [PT, NT])
        rstd = sb("rstd", [PT, NT])
        shift = sb("shift", [PT, NT])
        xn = sb("xn", [PT, NT, D])
        cf = sb("cf", [D, 2, HS])
        xf = sb("xf", [D, 2, HS])
        kf = sb("kf", [D, 2, HS])
        vf = sb("vf", [D, 2, HS])
        prod = sb("prod", [D, 2, 2, HS])
        rsb = sb("rsb", [PS, 2, 2 * HT, 2 * NH])
        corr_sb = sb("corr_sb", [D, 2, LF])
        top8 = sb("top8", [D, 2, 8])
        ntop = sb("ntop", [D, 2])
        cexp = sb("cexp", [D, 2, L])
        taken = sb("taken", [D, 2, LF])
        wraw = sb("wraw", [D, 2, L])
        wsum = sb("wsum", [D, 2])
        winv = sb("winv", [D, 2])
        wtau_t = sb("wtau_t", [L, 2, D])
        wown = sb("wown", [D, 2, NT, SP])
        t1 = sb("t1", [D, 2, HS])
        t2 = sb("t2", [D, 2, HS])
        of = sb("of", [D, 2, HS])
        y_sb = sb("y_sb", [PS, NT, D])
        x2 = sb("x2", [PT, NT, D])
        logit = sb("logit", [PT, NT, E])
        ltop = sb("ltop", [PT, NT, 8])
        ldif = sb("ldif", [PT, NT, E])
        lmask = sb("lmask", [PT, NT, E])
        ltanh = sb("ltanh", [PT, NT, E])
        lnum = sb("lnum", [PT, NT, E])
        lden = sb("lden", [PT, NT, E])
        lrec = sb("lrec", [PT, NT, E])
        lexp = sb("lexp", [PT, NT, E])
        lsum = sb("lsum", [PT, NT])
        linv = sb("linv", [PT, NT])
        route = sb("route", [PT, NT, E])
        route_t = sb("route_t", [E, 2, TOK])
        route_b = sb("route_b", [D, ROUTES, 2, TOK])
        wr2 = sb("wr2", [D, 2 * E], F32R)
        xth = sb("xth", [D, 2, TOK], F32R)
        xtl = sb("xtl", [D, 2, TOK], F32R)
        weh = sb("weh", [D, E, 2, H], F32R)
        wel = sb("wel", [D, E, 2, H], F32R)
        hid = prod[:, :, :, :].rearrange("p k a s -> p (k a s)")[:, 0:4 * TOK].rearrange("p (s a t) -> p s a t", s=2, a=2)
        hidh = sb("hidh", [D, SLOTS, 2, TOK], F32R)
        hidl = sb("hidl", [D, SLOTS, 2, TOK], F32R)
        scaled = kf[:, :, 0:TOK]
        acc = cf[:, :, 0:TOK]
        o_sb = sb("o_sb", [PT, NT, D])

        bank = stack.enter_context(nc.psum_tensor("bank", [D, 8, 512], F32))
        ident = tb[:, B_ID:B_ID + D]

        in_ta, in_tb, in_wa = sem("in_ta"), sem("in_tb"), sem("in_wa")
        in_c = [sem(f"in_c{half}") for half in range(2)]
        in_x = [sem(f"in_x{half}") for half in range(2)]
        in_rows, in_g, in_shared, in_cols = sem("in_rows"), sem("in_g"), sem("in_shared"), sem("in_cols")
        in_we = [sem(f"in_we{e}") for e in range(E)]
        dve = sem("dve_done")
        c_spec, cf_ok = sem("context_spectra"), sem("context_spectra_in_sbuf")
        norm_ok, xn_v, xn_s = sem("norm_factors"), sem("xn_by_vector"), sem("xn_by_scalar")
        x_spec, xf_ok = sem("x_spectra"), [sem("x_spectra_in_sbuf0"), sem("x_spectra_in_sbuf1")]
        k_proj, v_proj, q_proj = sem("k_projected"), sem("v_projected"), sem("q_projected")
        k_ok, v_ok = sem("k_in_sbuf"), sem("v_in_sbuf")
        prod_ok, heads, rsb_ok = sem("products_ready"), sem("head_sums"), sem("head_sums_in_sbuf")
        corr, ntop_ok, cexp_ok = sem("correlations"), sem("top_found"), sem("correlation_exponentials")
        wraw_ok, wt_mm, wt_ok = sem("shift_weights"), sem("shift_weights_transposed"), sem("shift_weights_t_in_sbuf")
        ws_mm, wown_ok, warm_ok = sem("weight_spectra"), sem("weight_spectra_in_their_columns"), sem("filler_cleared")
        wrep, of_ok = sem("weight_spectra_repeated"), sem("output_spectra")
        y_mm, y_ok, attn, x2_ok = sem("y_products"), sem("y_in_sbuf"), sem("attention_out"), sem("x2_ready")
        tanh_ok, xres_ok = sem("gates_ready"), sem("residual_with_bias")
        xt_mm, xth_ok, xt_ok = sem("x2_transposed"), sem("x2_lead"), sem("x2_split")
        wr_ok, logit_mm, ldif_ok, ltanh_ok = sem("router_split"), sem("logits"), sem("logit_differences"), sem("logit_tanh")
        route_ok, route_mm, route_sb, route_out = sem("routes"), sem("routes_transposed"), sem("routes_in_sbuf"), sem("routes_in_dram")
        in_route = [sem(f"route_weights_{e}") for e in range(E)]
        lead_s, lead_p, we_split, pool = sem("weights_lead_by_scalar"), sem("weights_lead_by_pool"), sem("weights_split"), sem("pool_done")
        h_mm, gelu_ok, hid_hi, hid_ok = sem("hidden_products"), sem("gelu_done"), sem("hidden_lead"), sem("hidden_split")
        y_expert, scaled_ok, acc_ok = sem("expert_products"), sem("expert_taken"), sem("experts_summed")
        last_half, sum_ok, back_mm, o_ok, stored = sem("last_expert_half"), sem("sum_complete"), sem("sum_transposed"), sem("result_ready"), sem("stored")

        BY_SCALAR = (2, 3, 6, 7)
        LEAD_BY_SCALAR = 2

        def spectra(t):
            return t.rearrange("p (b s f) -> p b s f", s=2, f=NF)

        def tiled(t):
            return t.rearrange("p (i d) -> p i d", d=D)

        def norm_counts(n, times):
            if n in BY_SCALAR:
                return xn_s, times * len(BY_SCALAR) + BY_SCALAR.index(n) + 1
            return xn_v, times * (NT - len(BY_SCALAR)) + [i for i in range(NT) if i not in BY_SCALAR].index(n) + 1

        IN_HALVES = (0, E * HC - 1)

        def parts(n):
            return [(0, slice(0, 1)), (1, slice(1, 2))] if n in IN_HALVES else [(0, slice(0, 2))]

        def upto(n, part=None):
            last = len(parts(n)) if part is None else part + 1
            return n + (1 if n > 0 else 0) + last

        block = stack.enter_context(nc.Block())

        @block.sync
        def _(sp):
            for half in range(2):
                tiles = slice(half * HT, (half + 1) * HT)
                sp.dma_start(x_sb[:, tiles, :], x[:, tiles, :]).then_inc(in_x[half], 16)
            sp.dma_start(c_sb[:, HT:NT, :], ctx[:, HT:NT, :]).then_inc(in_c[1], 16)
            sp.dma_start(rows_sb[:, :, :], bias_rows).then_inc(in_rows, 16)
            sp.dma_start(tb[:, :], tab_b).then_inc(in_tb, 16)
            for e in range(E):
                if e >= RING:
                    sp.wait_ge(we_split, 2 * (e - RING + 1))
                sp.dma_start(we_sb[:, e % RING, :, :], w_experts[e]).then_inc(in_we[e], 16)
            for half in range(2):
                sp.wait_ge(route_sb, half + 1)
                sp.dma_start(route_dram[:, half, :], route_t[:, half, :]).then_inc(route_out, 16)
            sp.wait_ge(route_out, 32)
            for e in range(E):
                if e >= ROUTES:
                    sp.wait_ge(scaled_ok, 2 * (e - ROUTES + 1))
                sp.dma_start(route_b[:, e % ROUTES, :, :], route_dram[e:e + 1].broadcast_to([D, 2, TOK])).then_inc(in_route[e], 16)
            for half in range(2):
                sp.wait_ge(o_ok, half + 1)
                tiles = slice(half * HT, (half + 1) * HT)
                sp.dma_start(out[:, tiles, :], o_sb[:, tiles, :]).then_inc(stored, 16)
            sp.wait_ge(stored, 32)

        @block.gpsimd
        def _(gp):
            gp.wait_ge(in_cols, 16)
            gp.tensor_copy(wr2[:, 0:E], col_sb[:, P_WR:P_WR + E]).then_inc(pool, 1)
            gp.wait_ge(pool, 1)
            gp.tensor_tensor(wr2[:, E:2 * E], col_sb[:, P_WR:P_WR + E], wr2[:, 0:E].bitcast(F32), ALU.subtract).then_inc(wr_ok, 1)
            gp.wait_ge(in_shared, 16)
            gp.wait_ge(tanh_ok, 1)
            gp.tensor_scalar(shared[:, 0:D], shared[:, 0:D], tanh_g[0:PT, 0:1], None, ALU.mult).then_inc(pool, 1)
            gp.wait_ge(pool, 2)
            gp.tensor_tensor(xres[:, :, :], x_sb[:, :, :], shared[:, 0:D].unsqueeze(1).broadcast_to([PT, NT, D]),
                             ALU.add).then_inc(xres_ok, 1)
            for e in range(E):
                gp.wait_ge(in_we[e], 16)
                for k in range(2):
                    if e < LEAD_BY_SCALAR:
                        gp.wait_ge(lead_s, 2 * e + k + 1)
                    else:
                        gp.tensor_copy(weh[:, e, k, :], we_sb[:, e % RING, k, :]).then_inc(lead_p, 1)
                        gp.wait_ge(lead_p, 2 * (e - LEAD_BY_SCALAR) + k + 1)
                    gp.tensor_tensor(wel[:, e, k, :], we_sb[:, e % RING, k, :], weh[:, e, k, :].bitcast(F32),
                                     ALU.subtract).then_inc(we_split, 1)
            for e in range(1, E - 1):
                for half in range(2):
                    gp.wait_ge(scaled_ok, 2 * e + half + 1)
                    gp.tensor_tensor(acc[:, half, :], acc[:, half, :], scaled[:, half, :], ALU.add).then_inc(acc_ok, 1)

        @block.scalar
        def _(act):
            act.dma_start(ta[:, :], tab_a).then_inc(in_ta, 16)
            act.dma_start(c_sb[:, 0:HT, :], ctx[:, 0:HT, :]).then_inc(in_c[0], 16)
            act.dma_start(wa_sb[:, :, :], w_attn).then_inc(in_wa, 16)
            act.preload_act_table(ACT.Exp)
            act.dma_start(g_sb[:, :], gates.broadcast_to([D, 2])).then_inc(in_g, 16)
            act.dma_start(col_sb[:, :], cols).then_inc(in_cols, 16)
            act.dma_start(shared[:, :], shared_rows.broadcast_to([PT, D + E])).then_inc(in_shared, 16)
            for half in range(2):
                act.wait_ge(c_spec, half + 1)
                act.copy(cf[:, half, :], bank[:, half, 0:HS]).then_inc(cf_ok, 1)

            def normalise(src, times, half):
                act.wait_ge(norm_ok, 2 * times + half + 1)
                for i in BY_SCALAR[half * len(BY_SCALAR) // 2:(half + 1) * len(BY_SCALAR) // 2]:
                    act.activation(xn[:, i, :], src[:, i, :], ACT.Identity, bias=shift[:, i:i + 1],
                                   scale=rstd[:, i:i + 1]).then_inc(xn_s, 1)

            def take(projected, spectrum, first, done, half):
                act.wait_ge(projected, half + 1)
                act.copy(spectrum[:, half, :], bank[:, first + half, 0:HS]).then_inc(done, 1)

            normalise(x_sb, 0, 0)
            take(k_proj, kf, 4, k_ok, 0)
            normalise(x_sb, 0, 1)
            take(k_proj, kf, 4, k_ok, 1)
            act.wait_ge(x_spec, 2)
            act.copy(xf[:, 1, :], bank[:, 3, 0:HS]).then_inc(xf_ok[1], 1)
            act.wait_ge(in_g, 16)
            act.activation(tanh_g[:, :], g_sb[:, :], ACT.Tanh).then_inc(tanh_ok, 1)
            def lead(e, k):
                act.wait_ge(in_we[e], 16)
                act.copy(weh[:, e, k, :], we_sb[:, e % RING, k, :]).then_inc(lead_s, 1)

            lead(0, 0)
            lead(0, 1)
            lead(1, 0)
            for t in range(2):
                act.wait_ge(ntop_ok, t + 1)
                act.activation(cexp[:, t, :], corr_sb[:, t, 0:L], ACT.Exp, bias=ntop[:, t:t + 1]).then_inc(cexp_ok, 1)
            take(v_proj, vf, 6, v_ok, 0)
            take(v_proj, vf, 6, v_ok, 1)
            act.preload_act_table(ACT.Gelu)
            lead(1, 1)
            for half in range(2):
                act.wait_ge(y_mm, half + 1)
                act.copy(y_sb[:, half * HT:(half + 1) * HT, :], tiled(bank[0:PS, 4 + half, :])).then_inc(y_ok, 1)
            for half in range(2):
                normalise(x2, 1, half)
                act.wait_ge(xt_mm, half + 1)
                act.copy(xth[:, half, :], bank[:, 6 + half, 0:TOK]).then_inc(xth_ok, 1)
            for n in range(E * HC):
                for part, halves in parts(n):
                    act.wait_ge(h_mm, upto(n, part))
                    if n >= 2:
                        act.wait_ge(hid_ok, upto(n - 2))
                    act.activation(hid[:, n % 2, halves, :], bank[:, 2 * (n % 2):2 * (n % 2) + 2, 0:TOK][:, halves, :], ACT.Gelu,
                                   bias=col_sb[:, P_B1 + n:P_B1 + n + 1]).then_inc(gelu_ok, 1)
                    act.wait_ge(gelu_ok, upto(n, part))
                    if n >= SLOTS:
                        act.wait_ge(y_expert, n - SLOTS + 1)
                    act.copy(hidh[:, n % SLOTS, halves, :], hid[:, n % 2, halves, :]).then_inc(hid_hi, 1)
                if n == 2:
                    act.wait_ge(ldif_ok, 1)
                    act.activation(ltanh[:, :, :], ldif[:, :, :], ACT.Tanh, scale=0.5).then_inc(ltanh_ok, 1)

        @block.vector
        def _(ve):
            count = [0]

            def mark(instruction):
                count[0] += 1
                instruction.then_inc(dve, 1)

            def settle():
                ve.wait_ge(dve, count[0])

            def link(instruction):
                mark(instruction)
                settle()

            ve.memset(filler[:, :], 0.0).then_inc(warm_ok, 1)

            def load(half):
                ve.wait_ge(in_x[half], 16)

            def residual(half):
                tiles = slice(half * HT, (half + 1) * HT)
                ve.wait_ge(attn, half + 1)
                link(ve.scalar_tensor_tensor(out=x2[:, tiles, :], in0=tiled(bank[0:PT, half, :]),
                                             scalar=tanh_g[0:PT, 0:1], in1=xres[:, tiles, :], op0=ALU.mult, op1=ALU.add))

            def moments(src, half, steps=range(2 * HT)):
                for k in steps:
                    i = half * HT + k % HT
                    if k == HT:
                        settle()
                    if k < HT:
                        mark(ve.bn_stats(stat[:, i, :], src[:, i, :]))
                    else:
                        mark(ve.bn_aggr(mv[:, i, :], stat[:, i, :]))

            def factors(half, step):
                c = slice(half * HT, (half + 1) * HT)
                ve.wait_ge(dve, reached[half])
                if step == 0:
                    mark(ve.tensor_scalar(var[:, c], mv[:, c, 1], EPS, None, ALU.add))
                elif step == 1:
                    mark(ve.tensor_scalar(rs_a[:, c].bitcast(I32), var[:, c].bitcast(I32), -0.5, GUESS, ALU.mult, ALU.add))
                elif step == 2:
                    mark(ve.tensor_tensor(rs_b[:, c], rs_a[:, c], rs_a[:, c], ALU.mult))
                elif step == 3:
                    mark(ve.scalar_tensor_tensor(out=rs_b[:, c], in0=rs_b[:, c], scalar=-STEP_A, in1=var[:, c],
                                                 op0=ALU.mult, op1=ALU.mult))
                elif step == 4:
                    mark(ve.scalar_tensor_tensor(out=rs_c[:, c], in0=rs_b[:, c], scalar=STEP_B, in1=rs_a[:, c],
                                                 op0=ALU.add, op1=ALU.mult))
                elif step == 5:
                    mark(ve.tensor_tensor(rs_b[:, c], rs_c[:, c], rs_c[:, c], ALU.mult))
                elif step == 6:
                    mark(ve.tensor_tensor(rs_b[:, c], rs_b[:, c], var[:, c], ALU.mult))
                elif step == 7:
                    mark(ve.tensor_scalar(rs_d[:, c], rs_b[:, c], 0.375, -1.25, ALU.mult, ALU.add))
                elif step == 8:
                    mark(ve.tensor_tensor(rs_d[:, c], rs_d[:, c], rs_b[:, c], ALU.mult))
                elif step == 9:
                    mark(ve.scalar_tensor_tensor(out=rstd[:, c], in0=rs_d[:, c], scalar=1.875, in1=rs_c[:, c],
                                                 op0=ALU.add, op1=ALU.mult))
                else:
                    ve.scalar_tensor_tensor(out=shift[:, c], in0=mv[:, c, 0], scalar=-1.0, in1=rstd[:, c],
                                            op0=ALU.mult, op1=ALU.mult).then_inc(norm_ok, 1)
                reached[half] = count[0]

            def apply(src, half):
                for i in range(half * HT, (half + 1) * HT):
                    if i not in BY_SCALAR:
                        ve.tensor_scalar(xn[:, i, :], src[:, i, :], mv[:, i, 0:1], rstd[:, i:i + 1],
                                         ALU.subtract, ALU.mult).then_inc(xn_v, 1)

            def normalise(src, begin):
                begin(0)
                moments(src, 0)
                reached[0] = count[0]
                factors(0, 0)
                factors(0, 1)
                begin(1)
                for step in range(2, RSTEPS):
                    if step - 2 < 2 * HT:
                        moments(src, 1, [step - 2])
                    factors(0, step)
                reached[1] = count[0]
                factors(1, 0)
                apply(src, 0)
                for step in range(1, RSTEPS):
                    factors(1, step)
                apply(src, 1)

            RSTEPS = 11
            reached = [0, 0]
            for t in range(2):
                ve.memset(corr_sb[:, t, L:LF], FILL)
            normalise(x_sb, load)
            ve.wait_ge(x_spec, 1)
            ve.tensor_copy(xf[:, 0, :], bank[:, 2, 0:HS]).then_inc(xf_ok[0], 1)
            for half in range(2):
                ve.wait_ge(q_proj, half + 1)
                ve.wait_ge(k_ok, half + 1)
                q_ps = bank[:, half, 0:HS]
                ve.tensor_tensor(prod[:, 0, half, :], q_ps, kf[:, half, :], ALU.mult).then_inc(prod_ok, 1)
                p2, q2, k2 = spectra(prod[:, 1, half, :]), spectra(q_ps), spectra(kf[:, half, :])
                for s in range(2):
                    ve.tensor_tensor(p2[:, :, s, :], q2[:, :, s, :], k2[:, :, 1 - s, :], ALU.mult).then_inc(prod_ok, 1)
            for half in range(2):
                ve.wait_ge(heads, half + 1)
                ve.tensor_tensor(rsb[:, half, :, :].rearrange("p i (n h) -> p i n h", n=2),
                                 bank[0:PS, 2 + half, 0:2 * HT * NH].rearrange("p (i h) -> p i h", h=NH)
                                 .unsqueeze(2).broadcast_to([PS, 2 * HT, 2, NH]),
                                 tb[0:PS, B_MASK:B_MASK + 2 * NH].rearrange("p (n h) -> p n h", n=2)
                                 .unsqueeze(1).broadcast_to([PS, 2 * HT, 2, NH]), ALU.mult).then_inc(rsb_ok, 1)
            for t in range(2):
                ve.wait_ge(corr, t + 1)
                mark(ve.max(top8[:, t, :], bank[:, 4 + t, 0:L]))
                mark(ve.tensor_copy(corr_sb[:, t, 0:L], bank[:, 4 + t, 0:L]))
            settle()
            for t in range(2):
                ve.tensor_scalar(ntop[:, t:t + 1], top8[:, t, 0:1], -1.0, None, ALU.mult).then_inc(ntop_ok, 1)
            mark(ve.memset(top8[:, :, TOP:8], FILL))
            settle()
            for t in range(2):
                mark(ve.match_replace(taken[:, t, :], top8[:, t, :], corr_sb[:, t, :], TAKEN))
            settle()
            for t in range(2):
                ve.wait_ge(cexp_ok, t + 1)
                ve.scalar_tensor_tensor(out=wraw[:, t, :], in0=taken[:, t, 0:L], scalar=TAKEN, in1=cexp[:, t, :],
                                        op0=ALU.is_equal, op1=ALU.mult).then_inc(wraw_ok, 1)
            ve.wait_ge(wraw_ok, 2)
            link(ve.tensor_reduce(wsum[:, :], wraw[:, :, :], AX.X, ALU.add))
            mark(ve.reciprocal(winv[:, :], wsum[:, :]))
            for t in range(2):
                ve.wait_ge(wt_mm, t + 1)
                ve.tensor_copy(wtau_t[:, t, :], bank[0:L, t, 0:D]).then_inc(wt_ok, 1)
            settle()
            for t in range(2):
                ve.wait_ge(ws_mm, t + 1)
                ve.scalar_tensor_tensor(out=wown[:, t, :, :], in0=bank[:, 4 + t, 0:SP].unsqueeze(1).broadcast_to([D, NT, SP]),
                                        scalar=winv[:, t:t + 1],
                                        in1=tb[:, B_OWN:B_OWN + NT].unsqueeze(2).broadcast_to([D, NT, SP]),
                                        op0=ALU.mult, op1=ALU.mult).then_inc(wown_ok, 1)
            for half in range(2):
                ve.wait_ge(wrep, half + 1)
                ve.wait_ge(v_ok, half + 1)
                ws = bank[:, 2 + half, 0:HS]
                wsv, v2, t1v, t2v, ov = (spectra(t) for t in (ws, vf[:, half, :], t1[:, half, :], t2[:, half, :], of[:, half, :]))
                mark(ve.tensor_tensor(t1[:, half, :], ws, vf[:, half, :], ALU.mult))
                for s in range(2):
                    mark(ve.tensor_tensor(t2v[:, :, s, :], wsv[:, :, s, :], v2[:, :, 1 - s, :], ALU.mult))
                settle()
                ve.tensor_tensor(ov[:, :, 0, :], t1v[:, :, 0, :], t1v[:, :, 1, :], ALU.add).then_inc(of_ok, 1)
                ve.tensor_tensor(ov[:, :, 1, :], t2v[:, :, 0, :], t2v[:, :, 1, :], ALU.subtract).then_inc(of_ok, 1)
            ve.wait_ge(xres_ok, 1)
            ve.wait_ge(tanh_ok, 1)
            ve.wait_ge(x_spec, 2)
            normalise(x2, residual)
            for half in range(2):
                ve.wait_ge(xth_ok, half + 1)
                ve.tensor_tensor(xtl[:, half, :], bank[:, 6 + half, 0:TOK], xth[:, half, :].bitcast(F32), ALU.subtract).then_inc(xt_ok, 1)

            def logit_differences():
                ve.wait_ge(in_shared, 16)
                ve.wait_ge(logit_mm, 1)
                lp = bank[0:PT, 4, 0:NT * 2 * E].rearrange("p (i e) -> p i e", e=2 * E)
                link(ve.tensor_tensor(logit[:, :, :], lp[:, :, 0:E], shared[:, D:D + E].unsqueeze(1).broadcast_to([PT, NT, E]), ALU.add))
                link(ve.tensor_tensor(logit[:, :, :], lp[:, :, E:2 * E], logit[:, :, :], ALU.add))
                for i in range(NT):
                    mark(ve.max(ltop[:, i, :], logit[:, i, :]))
                settle()
                ve.tensor_tensor(ldif[:, :, :], ltop[:, :, 0:1].broadcast_to([PT, NT, E]), logit[:, :, :],
                                 ALU.subtract).then_inc(ldif_ok, 1)
                mark(ve.tensor_tensor(lmask[:, :, :], logit[:, :, :], ltop[:, :, 1:2].broadcast_to([PT, NT, E]), ALU.is_ge))

            def routes():
                ve.wait_ge(ltanh_ok, 1)
                mark(ve.tensor_scalar(lnum[:, :, :], ltanh[:, :, :], -1.0, 1.0, ALU.mult, ALU.add))
                link(ve.tensor_scalar(lden[:, :, :], ltanh[:, :, :], 1.0, None, ALU.add))
                link(ve.reciprocal(lrec[:, :, :], lden[:, :, :]))
                link(ve.tensor_tensor(lexp[:, :, :], lnum[:, :, :], lrec[:, :, :], ALU.mult))
                link(ve.tensor_tensor(lexp[:, :, :], lexp[:, :, :], lmask[:, :, :], ALU.mult))
                link(ve.tensor_reduce(lsum[:, :], lexp[:, :, :], AX.X, ALU.add))
                link(ve.reciprocal(linv[:, :], lsum[:, :]))
                ve.tensor_tensor(route[:, :, :], lexp[:, :, :], linv[:, :].unsqueeze(2).broadcast_to([PT, NT, E]),
                                 ALU.mult).then_inc(route_ok, 1)

            def take_expert(e, half):
                if e < E - 1:
                    ve.wait_ge(y_expert, HC * (e + 1))
                    if e >= 2:
                        ve.wait_ge(acc_ok, 2 * (e - 2) + half + 1)
                else:
                    ve.wait_ge(last_half, half + 1)
                    ve.wait_ge(acc_ok, 2 * (e - 2) + half + 1)
                ve.wait_ge(in_route[e], 16)
                into = acc if e == 0 else scaled
                ve.scalar_tensor_tensor(out=into[:, half, :], in0=bank[:, 6 - 2 * (e % 2) + half, 0:TOK],
                                        scalar=col_sb[:, P_B2 + e:P_B2 + e + 1], in1=route_b[:, e % ROUTES, half, :],
                                        op0=ALU.add, op1=ALU.mult).then_inc(scaled_ok, 1)

            for n in range(E * HC):
                for part, halves in parts(n):
                    ve.wait_ge(hid_hi, upto(n, part))
                    if n >= SLOTS:
                        ve.wait_ge(y_expert, n - SLOTS + 1)
                    ve.tensor_tensor(hidl[:, n % SLOTS, halves, :], hid[:, n % 2, halves, :],
                                     hidh[:, n % SLOTS, halves, :].bitcast(F32), ALU.subtract).then_inc(hid_ok, 1)
                if n == 1:
                    logit_differences()
                if n == 2:
                    routes()
                if n == 3:
                    for half in range(2):
                        ve.wait_ge(route_mm, half + 1)
                        ve.tensor_copy(route_t[:, half, :], bank[0:E, 4 + half, 0:TOK]).then_inc(route_sb, 1)
                if n % HC in (2, 3) and n > HC:
                    take_expert(n // HC - 1, n % HC - 2)
            for half in range(2):
                take_expert(E - 1, half)
                ve.wait_ge(scaled_ok, 2 * (E - 1) + half + 1)
                ve.tensor_tensor(acc[:, half, :], acc[:, half, :], scaled[:, half, :], ALU.add).then_inc(sum_ok, 1)
            for half in range(2):
                tiles = slice(half * HT, (half + 1) * HT)
                ve.wait_ge(back_mm, half + 1)
                ve.scalar_tensor_tensor(out=o_sb[:, tiles, :], in0=tiled(bank[0:PT, half, :]),
                                        scalar=tanh_g[0:PT, 1:2], in1=x2[:, tiles, :], op0=ALU.mult, op1=ALU.add).then_inc(o_ok, 1)

        @block.tensor
        def _(pe):
            pe.wait_ge(warm_ok, 1)
            for k in range(WARM):
                pe.matmul(bank[:, 7, :], filler[:, 0:D], filler[:, :], start=True, stop=True)
            pe.wait_ge(in_ta, 16)

            def to_spectra(src, first, i):
                return pe.matmul(bank[:, first + i // HT, (i % HT) * PS:(i % HT + 1) * PS], src[:, i, :],
                                 ta[:, A_FWD:A_FWD + PS], start=(i % HT == 0), stop=(i % HT == HT - 1),
                                 skip_group_check=True)

            def project_spectra(k, first, src, projected, half):
                pe.matmul(bank[:, first + half, 0:HS], wa_sb[:, k, :], src[:, half, :], start=True, stop=False,
                          skip_group_check=True)
                pe.matmul(spectra(bank[:, first + half, 0:HS])[:, :, 0, 0], rows_sb[:, k, :], ta[0:1, A_DC:A_DC + NT],
                          start=False, stop=True, skip_group_check=True).then_inc(projected, 1)

            for i in range(NT):
                pe.wait_ge(in_c[i // HT], 16)
                mm = to_spectra(c_sb, 0, i)
                if i % HT == HT - 1:
                    mm.then_inc(c_spec, 1)
            pe.wait_ge(in_wa, 16)
            pe.wait_ge(in_rows, 16)
            for half in range(2):
                pe.wait_ge(cf_ok, half + 1)
                project_spectra(1, 4, cf, k_proj, half)
            for i in range(NT):
                pe.wait_ge(*norm_counts(i, 0))
                mm = to_spectra(xn, 2, i)
                if i % HT == HT - 1:
                    mm.then_inc(x_spec, 1)
            for half in range(2):
                pe.wait_ge(xf_ok[half], 1)
                project_spectra(0, 0, xf, q_proj, half)
            pe.wait_ge(in_tb, 16)
            for half in range(2):
                for kind in range(2):
                    pe.wait_ge(prod_ok, 3 * half + 1 + 2 * kind)
                    for i in range(HT):
                        at = (kind * HT + i) * NH
                        mm = pe.matmul(bank[0:PS, 2 + half, at:at + NH], prod[:, kind, half, i * PS:(i + 1) * PS],
                                       tb[:, B_SUM:B_SUM + NH], start=(kind == 0 and i == 0), stop=True,
                                       skip_group_check=True)
                mm.then_inc(heads, 1)
            for t in range(2):
                pe.wait_ge(rsb_ok, t + 1)
                for j in range(HT):
                    for kind in range(2):
                        mm = pe.matmul(bank[32 * j:32 * j + 32, 4 + t, 0:L], rsb[:, t, kind * HT + j, :],
                                       tb[0:PS, B_INV + kind * L:B_INV + (kind + 1) * L],
                                       start=(kind == 0), stop=(kind == 1), skip_group_check=True,
                                       tile_position=(0, 32 * j))
                mm.then_inc(corr, 1)
            for half in range(2):
                project_spectra(2, 6, cf, v_proj, half)
            for t in range(2):
                pe.wait_ge(wraw_ok, t + 1)
                pe.transpose(bank[0:L, t, 0:D], wraw[:, t, :], ident).then_inc(wt_mm, 1)
            for t in range(2):
                pe.wait_ge(wt_ok, t + 1)
                pe.matmul(bank[:, 4 + t, 0:SP], wtau_t[:, t, :], tb[0:L, B_FWD1:B_FWD1 + SP], start=True, stop=True).then_inc(ws_mm, 1)
            for t in range(2):
                pe.wait_ge(wown_ok, t + 1)
                pe.matmul(bank[:, 2 + t, 0:HS], tb[:, B_REP:B_REP + D], wown[:, t, :, :].rearrange("p b f -> p (b f)"),
                          start=True, stop=True).then_inc(wrep, 1)
            for half in range(2):
                pe.wait_ge(of_ok, 2 * half + 2)
                for i in range(HT):
                    mm = pe.matmul(bank[0:PS, 4 + half, i * D:(i + 1) * D], of[:, half, i * PS:(i + 1) * PS], wa_sb[:, 3, :],
                                   start=(i == 0), stop=(i == HT - 1), skip_group_check=True)
                mm.then_inc(y_mm, 1)
            for half in range(2):
                pe.wait_ge(y_ok, half + 1)
                pe.matmul(bank[0:PT, half, :], tb[0:PS, B_OUT:B_OUT + PT],
                          y_sb[:, half * HT:(half + 1) * HT, :].rearrange("p i d -> p (i d)"), start=True, stop=True).then_inc(attn, 1)
            for i in range(NT):
                pe.wait_ge(*norm_counts(i, 1))
                mm = pe.transpose(bank[:, 6 + i // HT, (i % HT) * PT:(i % HT + 1) * PT], xn[:, i, :], ident[0:PT, 0:PT])
                if i % HT == HT - 1:
                    mm.then_inc(xt_mm, 1)

            def hidden(n):
                e, c, slot = n // HC, n % HC, n % 2
                if c == 0:
                    pe.wait_ge(we_split, 2 * e + 1)
                if n >= 2:
                    pe.wait_ge(gelu_ok, upto(n - 2))
                cols_ = slice(c * D, (c + 1) * D)
                operands = ((weh, xth), (wel, xth), (weh, xtl))
                for part, halves in parts(n):
                    for k, (w, t) in enumerate(operands):
                        for half in range(halves.start, halves.stop):
                            if n == 0:
                                pe.wait_ge(xt_ok if k == 2 else xth_ok, half + 1)
                            mm = pe.matmul(bank[:, 2 * slot + half, 0:TOK], w[:, e, 0, cols_], t[:, half, :],
                                           start=(k == 0), stop=(k == 2))
                    mm.then_inc(h_mm, 1)

            def logits():
                pe.wait_ge(wr_ok, 1)
                for i in range(NT):
                    cols_ = slice((i % HT) * PT, (i % HT + 1) * PT)
                    at = i * 2 * E
                    pe.matmul(bank[0:PT, 4, at:at + 2 * E], xth[:, i // HT, cols_], wr2[:, :],
                              start=(i == 0), stop=False, skip_group_check=True)
                    mm = pe.matmul(bank[0:PT, 4, at:at + E], xtl[:, i // HT, cols_], wr2[:, 0:E],
                                   start=False, stop=(i == NT - 1), skip_group_check=True)
                mm.then_inc(logit_mm, 1)

            def turn_routes():
                pe.wait_ge(route_ok, 1)
                for i in range(NT):
                    at = (i % HT) * PT
                    mm = pe.transpose(bank[0:E, 4 + i // HT, at:at + PT], route[:, i, :], ident[0:PT, 0:PT])
                    if i % HT == HT - 1:
                        mm.then_inc(route_mm, 1)

            def project(n):
                e, c, slot = n // HC, n % HC, n % SLOTS
                if c == 0:
                    pe.wait_ge(we_split, 2 * e + 2)
                    if e == 1:
                        pe.wait_ge(route_sb, 2)
                    if e >= 2:
                        pe.wait_ge(scaled_ok, 2 * (e - 1))
                w_of = lambda w: w[:, e, 1, c * D:(c + 1) * D]
                operands = ((weh, hidh), (wel, hidh), (weh, hidl))
                pairs = [(k, half) for k in range(3) for half in range(2)]
                if n == E * HC - 1:
                    pairs = [(k, half) for half in range(2) for k in range(3)]
                for k, half in pairs:
                    pe.wait_ge(hid_ok if k == 2 else hid_hi, upto(n, half if n in IN_HALVES else 0))
                    mm = pe.matmul(bank[:, 6 - 2 * (e % 2) + half, 0:TOK], w_of(operands[k][0]), operands[k][1][:, slot, half, :],
                                   start=(c == 0 and k == 0), stop=(c == HC - 1 and k == 2))
                    if n == E * HC - 1 and k == 2:
                        mm.then_inc(last_half, 1)
                if n < E * HC - 1:
                    mm.then_inc(y_expert, 1)

            hidden(0)
            hidden(1)
            for n in range(E * HC):
                if n + 2 < E * HC:
                    hidden(n + 2)
                if n == 0:
                    logits()
                if n == 2:
                    turn_routes()
                project(n)
            for i in range(NT):
                half = i // HT
                if i % HT == 0:
                    pe.wait_ge(sum_ok, half + 1)
                mm = pe.transpose(bank[0:PT, half, (i % HT) * D:(i % HT + 1) * D], acc[:, half, (i % HT) * PT:(i % HT + 1) * PT], ident)
                if i % HT == HT - 1:
                    mm.then_inc(back_mm, 1)


def kernel(**inputs):
    import numpy as _np
    import concourse.bacc as _bacc
    from concourse import mybir as _mybir
    from concourse.bass_utils import run_bass_kernel_spmd as _run

    a = {n: _np.asarray(v) for n, v in inputs.items()}
    att, ffn = (lambda n: a["L0_xattn_" + n]), (lambda n: a["L0_ffn_" + n])

    def token_tiles(t):
        return t.reshape(NT, PT, D).transpose(1, 0, 2)

    w1 = ffn("W1").reshape(E, D, 1, H)
    w2 = ffn("W2").reshape(E, HC, D, D).transpose(0, 2, 1, 3).reshape(E, D, 1, H)
    tab_a, tab_b = tables()
    laid = {
        "x": token_tiles(a["x"]),
        "ctx": token_tiles(a["ctx_1024"][:, :L]),
        "w_attn": _np.stack([att("Wq"), att("Wk"), att("Wv"), att("Wo")], 1),
        "bias_rows": _np.stack([att("bq"), att("bk"), att("bv")])[None],
        "gates": _np.stack([a["g_xattn"], a["g_ffn"]], 1),
        "shared_rows": _np.concatenate([att("bo"), ffn("br")])[None],
        "cols": _np.concatenate([ffn("b2").T, ffn("b1").reshape(E * HC, D).T, ffn("Wr")], 1),
        "w_experts": _np.concatenate([w1, w2], 2),
        "tab_a": tab_a,
        "tab_b": tab_b,
    }
    nc = _bacc.Bacc("TRN2", target_bir_lowering=False, num_devices=1)
    arrays, args = {}, []
    for name, v in laid.items():
        v = _np.ascontiguousarray(v)
        arrays[f"in_{name}"] = v
        args.append(nc.dram_tensor(f"in_{name}", v.shape, _mybir.dt.from_np(v.dtype), kind="ExternalInput").ap())
    out = nc.dram_tensor("out_0", (PT, NT, D), _mybir.dt.float32, kind="ExternalOutput").ap()
    route = nc.dram_tensor("route_scratch", (E, 2, TOK), _mybir.dt.float32, kind="Internal").ap()
    build(nc, *args, out, route)
    got = _run(nc, [arrays], core_ids=[0]).results[0]["out_0"]
    return got.transpose(1, 0, 2).reshape(B, L, D)
```

```python
from contextlib import ExitStack

import numpy as np

import concourse.bass as bass
from concourse import mybir

F32 = mybir.dt.float32
F32R = mybir.dt.float32r
BF16 = mybir.dt.bfloat16
I32 = mybir.dt.int32
ALU = mybir.AluOpType
ACT = mybir.ActivationFunctionType
AX = mybir.AxisListType

B, L, D = 16, 56, 128
NH = 16
DK = D // NH
TOP = 4
LF = L + 8 - TOP
FILL, TAKEN = 3.0e38, -3.0e38
E, H = 8, 512
ROUTES = 3
HC = H // D
RING = 2
FILL_START, FILL_TOP, FILL_STEP, FILL_NORM = 9, 4, 2, 4
SLOTS = 3
NT = B // 2
PT = 2 * L
NF = L // 2 + 1
SP = 2 * NF
PS = 2 * SP
HT = NT // 2
HS = HT * PS
TOK = HT * PT
EPS = 1e-5
GUESS = float(0x5F1FFFF9)
STEP_A, STEP_B = 0.703952253, 0.703952253 * 2.38924456

A_FWD = 0
A_DC = A_FWD + PS
TAB_A = A_DC + NT
B_SUM = 0
B_INV = B_SUM + NH
B_MASK = B_INV + L
B_FWD1 = B_MASK + 2 * NH
B_IOTA = B_FWD1 + SP
B_OUT = B_IOTA + L
B_ID = B_OUT + PT
B_REP = B_ID + D
B_OWN = B_REP + D
TAB_B = B_OWN + NT
P_B2, P_B1, P_WR = 0, E, E + E * HC
PCOLS = P_WR + E


def tables():
    pos, freq, part = np.arange(L), np.arange(NF), np.arange(D)
    angle = 2 * np.pi * ((pos[:, None] * freq[None, :]) % L) / L
    cos, sin = np.cos(angle), np.sin(angle)
    fwd = np.concatenate([cos, sin], 1)
    both = np.where((freq == 0) | (freq == L // 2), 1.0, 2.0)[:, None]
    a, b = np.zeros((PT, TAB_A)), np.zeros((D, TAB_B))
    a[:L, A_FWD:A_FWD + SP] = fwd
    a[L:PT, A_FWD + SP:A_FWD + PS] = fwd
    a[0, A_DC:] = L
    b[:, B_SUM:B_SUM + NH] = part[:, None] // DK == np.arange(NH)
    back = np.concatenate([both * cos.T, both * sin.T]) / L
    for n in range(2):
        rows = slice(n * SP, (n + 1) * SP)
        b[rows, B_INV:B_INV + L] = back / DK
        b[rows, B_MASK + n * NH:B_MASK + (n + 1) * NH] = 1.0
        b[rows, B_OUT + n * L:B_OUT + (n + 1) * L] = back
    b[:L, B_FWD1:B_FWD1 + SP] = fwd
    b[:, B_IOTA:B_IOTA + L] = pos
    b[:, B_ID:B_ID + D] = np.eye(D)
    b[:, B_REP:B_REP + D] = part[:, None] % NH == part[None, :] // DK
    b[:, B_OWN:B_OWN + NT] = part[:, None] // NH == np.arange(NT)
    return a.astype(np.float32), b.astype(np.float32)


def build(nc, x, tab_ctx, w_attn, bias_rows, gates, shared_rows, cols, w_experts, tab_b, out, route_dram):
    with ExitStack() as stack:
        def sb(name, shape, dt=F32):
            return stack.enter_context(nc.sbuf_tensor(name, shape, dt))

        def sem(name):
            return stack.enter_context(nc.semaphore(name))

        ta_c = sb("ta_c", [PT, TAB_A + NT * D])
        ta = ta_c[:, 0:TAB_A]
        c_sb = ta_c[:, TAB_A:TAB_A + NT * D].rearrange("p (i d) -> p i d", d=D)
        tb = sb("tb", [D, TAB_B])
        x_sb = sb("x_sb", [PT, NT, D])
        wa_sb = sb("wa_sb", [D, 4, D])
        rows_sb = sb("rows_sb", [1, 3, D])
        shared = sb("shared", [PT, D + E])
        g_sb = sb("g_sb", [D, 2])
        col_sb = sb("col_sb", [D, PCOLS])
        we_sb = sb("we_sb", [D, RING, 2, H])
        filler = sb("filler", [D, 512], BF16)
        tanh_g = sb("tanh_g", [D, 2])
        xres = sb("xres", [PT, NT, D])
        stat = sb("stat", [PT, NT, 6])
        mv = sb("mv", [PT, NT, 2])
        var = sb("var", [PT, NT])
        rs_a = sb("rs_a", [PT, NT])
        rs_b = sb("rs_b", [PT, NT])
        rs_c = sb("rs_c", [PT, NT])
        rs_d = sb("rs_d", [PT, NT])
        rstd = sb("rstd", [PT, NT])
        shift = sb("shift", [PT, NT])
        xn = sb("xn", [PT, NT, D])
        cf = sb("cf", [D, 2, HS])
        xf = sb("xf", [D, 2, HS])
        kf = sb("kf", [D, 2, 2, HS])
        vf = sb("vf", [D, 2, 2, HS])
        prod = sb("prod", [D, 2, 2, HS])
        qk = sb("qk", [D, 2, HS])
        rsb = sb("rsb", [PS, NT, 2 * NH])
        corr_sb = sb("corr_sb", [D, 2, LF])
        top8 = sb("top8", [D, 2, 8])
        ntop = sb("ntop", [D, 2])
        cexp = sb("cexp", [D, 2, L])
        taken = sb("taken", [D, 2, LF])
        wraw = sb("wraw", [D, 2, L])
        wsum = sb("wsum", [D, 2])
        winv = sb("winv", [D, 2])
        wtau_t = sb("wtau_t", [L, 2, D])
        wown = sb("wown", [D, 2, NT, SP])
        tw = sb("tw", [D, 2, 2, HS])
        of = sb("of", [D, 2, HS])
        y_sb = sb("y_sb", [PS, NT, D])
        x2 = sb("x2", [PT, NT, D])
        logit = sb("logit", [PT, NT, E])
        ltop = sb("ltop", [PT, NT, 8])
        ldif = sb("ldif", [PT, NT, E])
        lmask = sb("lmask", [PT, NT, E])
        ltanh = sb("ltanh", [PT, NT, E])
        lnum = sb("lnum", [PT, NT, E])
        lden = sb("lden", [PT, NT, E])
        lrec = sb("lrec", [PT, NT, E])
        lexp = sb("lexp", [PT, NT, E])
        lsum = sb("lsum", [PT, NT])
        linv = sb("linv", [PT, NT])
        route = sb("route", [PT, NT, E])
        route_t = sb("route_t", [E, 2, TOK])
        route_b = sb("route_b", [D, ROUTES, 2, TOK])
        centre = sb("centre", [D, D])
        wrc = sb("wrc", [D, E])
        xth = sb("xth", [D, 2, TOK], F32R)
        xtl = sb("xtl", [D, 2, TOK], F32R)
        weh = sb("weh", [D, E, 2, H], F32R)
        wel = sb("wel", [D, E, 2, H], F32R)
        hid = prod[:, :, :, :].rearrange("p k a s -> p (k a s)")[:, 0:4 * TOK].rearrange("p (s a t) -> p s a t", s=2, a=2)
        hidh = sb("hidh", [D, SLOTS, 2, TOK], F32R)
        hidl = sb("hidl", [D, SLOTS, 2, TOK], F32R)
        scaled = kf[:, :, 0, 0:TOK]
        acc = cf[:, :, 0:TOK]
        x2t = xf[:, :, 0:TOK]
        o_sb = sb("o_sb", [PT, NT, D])

        bank = stack.enter_context(nc.psum_tensor("bank", [D, 8, 512], F32))
        ident = tb[:, B_ID:B_ID + D]

        in_tb, in_wa = sem("in_tb"), sem("in_wa")
        in_c = [sem(f"in_c{half}") for half in range(2)]
        in_x = [sem(f"in_x{half}") for half in range(2)]
        in_rows, in_g, in_shared, in_cols = sem("in_rows"), sem("in_g"), sem("in_shared"), sem("in_cols")
        in_we = [sem(f"in_we{e}") for e in range(E)]
        dve = sem("dve_done")
        c_spec, cf_ok = sem("context_spectra"), sem("context_spectra_in_sbuf")
        norm_ok, xn_v, xn_s = sem("norm_factors"), sem("xn_by_vector"), sem("xn_by_scalar")
        x_spec, xf_ok = sem("x_spectra"), [sem("x_spectra_in_sbuf0"), sem("x_spectra_in_sbuf1")]
        k_proj, v_proj, q_proj = sem("k_projected"), sem("v_projected"), sem("q_projected")
        k_ok, v_ok = sem("k_in_sbuf"), sem("v_in_sbuf")
        qk_mul, heads, rsb_ok = sem("queries_times_keys"), sem("head_sums"), sem("head_sums_in_sbuf")
        corr, ntop_ok, cexp_ok = sem("correlations"), sem("top_found"), sem("correlation_exponentials")
        wraw_ok, wt_mm, wt_ok = sem("shift_weights"), sem("shift_weights_transposed"), sem("shift_weights_t_in_sbuf")
        ws_mm, wown_ok, warm_ok = sem("weight_spectra"), sem("weight_spectra_in_their_columns"), sem("filler_cleared")
        wrep, of_mul = sem("weight_spectra_repeated"), sem("weights_times_values")
        qk_ok = [sem(f"cross_spectra{half}") for half in range(2)]
        of_ok = [sem(f"output_spectra{half}") for half in range(2)]
        stat_ok = sem("statistics")
        y_mm, y_ok, attn, x2_ok = sem("y_products"), sem("y_in_sbuf"), sem("attention_out"), sem("x2_ready")
        tanh_ok, xres_ok = sem("gates_ready"), sem("residual_with_bias")
        xt_mm, xth_ok, xt_ok = sem("x2_transposed"), sem("x2_lead"), sem("x2_split")
        centre_ok, wrc_mm, wrc_ok = sem("centring_matrix_ready"), sem("router_centred"), sem("router_centred_in_sbuf")
        logit_mm, ldif_ok, ltanh_ok = sem("logits"), sem("logit_differences"), sem("logit_tanh")
        route_ok, route_mm, route_sb, route_out = sem("routes"), sem("routes_transposed"), sem("routes_in_sbuf"), sem("routes_in_dram")
        in_route = [sem(f"route_weights_{e}") for e in range(E)]
        lead_s, lead_p, we_split, pool = sem("weights_lead_by_scalar"), sem("weights_lead_by_pool"), sem("weights_split"), sem("pool_done")
        h_mm, gelu_ok, hid_hi, hid_ok = sem("hidden_products"), sem("gelu_done"), sem("hidden_lead"), sem("hidden_split")
        x2t_mm, x2t_ok, x2_in = sem("x2_turned"), sem("x2_turned_in_sbuf"), sem("x2_in_the_sum")
        y_expert, scaled_ok, acc_ok = sem("expert_products"), sem("expert_taken"), sem("experts_summed")
        last_half, sum_v, sum_p = sem("last_expert_half"), sem("sum_complete_by_vector"), sem("sum_complete_by_pool")
        back_mm, o_s, o_v, stored = sem("sum_transposed"), sem("result_by_scalar"), sem("result_by_vector"), sem("stored")

        BY_SCALAR = ((3, 6, 7), (3, 6))
        LEAD_BY_SCALAR = 2

        def spectra(t):
            return t.rearrange("p (b s f) -> p b s f", s=2, f=NF)

        def tiled(t):
            return t.rearrange("p (i d) -> p i d", d=D)

        def norm_counts(n, times):
            before = sum(len(tiles) for tiles in BY_SCALAR[:times])
            if n in BY_SCALAR[times]:
                return xn_s, before + BY_SCALAR[times].index(n) + 1
            return xn_v, times * NT - before + [i for i in range(NT) if i not in BY_SCALAR[times]].index(n) + 1

        IN_HALVES = (0, E * HC - 1)

        def parts(n):
            return [(0, slice(0, 1)), (1, slice(1, 2))] if n in IN_HALVES else [(0, slice(0, 2))]

        def upto(n, part=None):
            last = len(parts(n)) if part is None else part + 1
            return n + (1 if n > 0 else 0) + last

        def add_products(engine, products, out_, done, kinds=(0, 1)):
            for kind in kinds:
                p = spectra(products[:, kind, :])
                engine.tensor_tensor(spectra(out_)[:, :, kind, :], p[:, :, 0, :], p[:, :, 1, :], ALU.add).then_inc(done, 1)

        block = stack.enter_context(nc.Block())

        @block.sync
        def _(sp):
            mid = TAB_A + HT * D
            sp.dma_start(x_sb[:, 0:HT, :], x[:, 0:HT, :]).then_inc(in_x[0], 16)
            sp.dma_start(ta_c[:, 0:mid], tab_ctx[:, 0:mid]).then_inc(in_c[0], 16)
            sp.dma_start(wa_sb[:, :, :], w_attn).then_inc(in_wa, 16)
            sp.dma_start(rows_sb[:, :, :], bias_rows).then_inc(in_rows, 16)
            sp.dma_start(tb[:, :], tab_b).then_inc(in_tb, 16)

            def load_expert(e):
                if e >= RING:
                    sp.wait_ge(we_split, 2 * (e - RING + 1))
                sp.dma_start(we_sb[:, e % RING, :, :], w_experts[e]).then_inc(in_we[e], 16)

            for e in range(E - 1):
                load_expert(e)
            sp.wait_ge(route_sb, 2)
            sp.dma_start(route_dram, route_t[:, :, :]).then_inc(route_out, 16)
            sp.wait_ge(route_out, 16)
            for e in range(E):
                if e == ROUTES:
                    load_expert(E - 1)
                if e >= ROUTES:
                    sp.wait_ge(scaled_ok, 2 * (e - ROUTES + 1))
                sp.dma_start(route_b[:, e % ROUTES, :, :], route_dram[e:e + 1].broadcast_to([D, 2, TOK])).then_inc(in_route[e], 16)
            for half in range(2):
                sp.wait_ge(o_s, half + 1)
                if half == 1:
                    sp.wait_ge(o_v, 1)
                tiles = slice(half * HT, (half + 1) * HT)
                sp.dma_start(out[:, tiles, :], o_sb[:, tiles, :]).then_inc(stored, 16)
            sp.wait_ge(stored, 32)

        @block.gpsimd
        def _(gp):
            gp.wait_ge(in_tb, 16)
            gp.tensor_scalar(centre[:, :], ident, 1.0 / D, None, ALU.subtract).then_inc(centre_ok, 1)
            gp.wait_ge(qk_mul, 1)
            add_products(gp, prod[:, 0, :, :], qk[:, 0, :], qk_ok[0])
            gp.wait_ge(in_shared, 16)
            gp.wait_ge(tanh_ok, 1)
            gp.tensor_scalar(shared[:, 0:D], shared[:, 0:D], tanh_g[0:PT, 0:1], None, ALU.mult).then_inc(pool, 1)
            gp.wait_ge(pool, 1)
            gp.tensor_tensor(xres[:, :, :], x_sb[:, :, :], shared[:, 0:D].unsqueeze(1).broadcast_to([PT, NT, D]),
                             ALU.add).then_inc(xres_ok, 1)
            for e in range(E):
                gp.wait_ge(in_we[e], 16)
                for k in range(2):
                    if e < LEAD_BY_SCALAR:
                        gp.wait_ge(lead_s, 2 * e + k + 1)
                    else:
                        gp.tensor_copy(weh[:, e, k, :], we_sb[:, e % RING, k, :]).then_inc(lead_p, 1)
                        gp.wait_ge(lead_p, 2 * (e - LEAD_BY_SCALAR) + k + 1)
                    gp.tensor_tensor(wel[:, e, k, :], we_sb[:, e % RING, k, :], weh[:, e, k, :].bitcast(F32),
                                     ALU.subtract).then_inc(we_split, 1)
                if e == 0:
                    for half in range(2):
                        gp.wait_ge(of_mul, 2 * half + 1)
                        add_products(gp, tw[:, half, :, :], of[:, half, :], of_ok[half], kinds=(0,))
            for e in range(1, E - 1):
                for half in range(2):
                    gp.wait_ge(scaled_ok, 2 * e + half + 1)
                    gp.tensor_tensor(acc[:, half, :], acc[:, half, :], scaled[:, half, :], ALU.add).then_inc(acc_ok, 1)
                    if e == 1:
                        gp.wait_ge(x2t_ok, half + 1)
                        gp.wait_ge(acc_ok, half + 1)
                        gp.tensor_tensor(acc[:, half, :], acc[:, half, :], x2t[:, half, :], ALU.add).then_inc(x2_in, 1)
                        gp.wait_ge(x2_in, half + 1)
            for half in range(2):
                gp.wait_ge(scaled_ok, 2 * (E - 1) + half + 1)
                gp.wait_ge(acc_ok, 2 * (E - 2))
                gp.tensor_tensor(acc[:, half, TOK // 2:], acc[:, half, TOK // 2:], scaled[:, half, TOK // 2:], ALU.add).then_inc(sum_p, 1)

        @block.scalar
        def _(act):
            act.dma_start(x_sb[:, HT:NT, :], x[:, HT:NT, :]).then_inc(in_x[1], 16)
            act.dma_start(ta_c[:, TAB_A + HT * D:], tab_ctx[:, TAB_A + HT * D:]).then_inc(in_c[1], 16)
            act.preload_act_table(ACT.Exp)
            act.dma_start(g_sb[:, :], gates.broadcast_to([D, 2])).then_inc(in_g, 16)
            act.dma_start(col_sb[:, :], cols).then_inc(in_cols, 16)
            act.dma_start(shared[:, :], shared_rows.broadcast_to([PT, D + E])).then_inc(in_shared, 16)
            for half in range(2):
                act.wait_ge(c_spec, half + 1)
                act.copy(cf[:, half, :], bank[:, half, 0:HS]).then_inc(cf_ok, 1)

            def normalise(src, times, tiles):
                act.wait_ge(norm_ok, times + 1)
                for i in tiles:
                    act.activation(xn[:, i, :], src[:, i, :], ACT.Identity, bias=shift[:, i:i + 1],
                                   scale=rstd[:, i:i + 1]).then_inc(xn_s, 1)

            def take(projected, first, spectrum, negated, done, half):
                act.wait_ge(projected, half + 1)
                src, changed = bank[:, first + half, 0:HS], spectra(spectrum[:, half, 1, :])
                act.copy(spectrum[:, half, 0, :], src)
                act.copy(changed[:, :, negated, :], spectra(src)[:, :, 1 - negated, :])
                act.activation(changed[:, :, 1 - negated, :], spectra(src)[:, :, negated, :], ACT.Copy,
                               scale=-1.0).then_inc(done, 1)

            normalise(x_sb, 0, BY_SCALAR[0][:1])
            take(k_proj, 4, kf, 1, k_ok, 0)
            normalise(x_sb, 0, BY_SCALAR[0][1:])
            act.wait_ge(x_spec, 2)
            act.copy(xf[:, 1, :], bank[:, 3, 0:HS]).then_inc(xf_ok[1], 1)
            take(k_proj, 4, kf, 1, k_ok, 1)
            act.wait_ge(in_g, 16)
            act.activation(tanh_g[:, :], g_sb[:, :], ACT.Tanh).then_inc(tanh_ok, 1)
            def lead(e, k):
                act.wait_ge(in_we[e], 16)
                act.copy(weh[:, e, k, :], we_sb[:, e % RING, k, :]).then_inc(lead_s, 1)

            lead(0, 0)
            lead(0, 1)
            take(v_proj, 6, vf, 0, v_ok, 0)
            take(v_proj, 6, vf, 0, v_ok, 1)
            for t in range(2):
                act.wait_ge(ntop_ok, t + 1)
                act.activation(cexp[:, t, :], corr_sb[:, t, 0:L], ACT.Exp, bias=ntop[:, t:t + 1]).then_inc(cexp_ok, 1)
            act.preload_act_table(ACT.Gelu)
            act.wait_ge(wrc_mm, 1)
            act.copy(wrc[:, :], bank[:, 6, 0:E]).then_inc(wrc_ok, 1)
            lead(1, 0)
            lead(1, 1)
            for half in range(2):
                act.wait_ge(y_mm, half + 1)
                act.activation(y_sb[:, half * HT:(half + 1) * HT, :], tiled(bank[0:PS, 4 + half, :]), ACT.Copy,
                               scale=tanh_g[0:PS, 0:1]).then_inc(y_ok, 1)
            for half in range(2):
                act.wait_ge(stat_ok, NT + HT * (half + 1))
                act.copy(x2[:, half * HT:(half + 1) * HT, :], tiled(bank[0:PT, half, :])).then_inc(x2_ok, 1)
            for half in range(2):
                act.wait_ge(x2t_mm, half + 1)
                act.copy(x2t[:, half, :], bank[:, 4 + half, 0:TOK]).then_inc(x2t_ok, 1)
            act.wait_ge(x2_ok, 2)
            normalise(x2, 1, BY_SCALAR[1])
            for half in range(2):
                act.wait_ge(xt_mm, half + 1)
                act.copy(xth[:, half, :], bank[:, 6 + half, 0:TOK]).then_inc(xth_ok, 1)
            def gelu(n, part, halves):
                act.wait_ge(h_mm, upto(n, part))
                if n >= 2:
                    act.wait_ge(hid_ok, upto(n - 2))
                act.activation(hid[:, n % 2, halves, :], bank[:, 2 * (n % 2):2 * (n % 2) + 2, 0:TOK][:, halves, :], ACT.Gelu,
                               bias=col_sb[:, P_B1 + n:P_B1 + n + 1]).then_inc(gelu_ok, 1)

            def lead_of_hidden(n, part, halves):
                act.wait_ge(gelu_ok, upto(n, part))
                if n >= SLOTS:
                    act.wait_ge(y_expert, n - SLOTS + 1)
                act.copy(hidh[:, n % SLOTS, halves, :], hid[:, n % 2, halves, :]).then_inc(hid_hi, 1)

            for n in range(E * HC):
                if n == 0:
                    for part, halves in parts(n):
                        gelu(n, part, halves)
                    for part, halves in parts(n):
                        lead_of_hidden(n, part, halves)
                else:
                    for part, halves in parts(n):
                        gelu(n, part, halves)
                        lead_of_hidden(n, part, halves)
                if n == 1:
                    act.wait_ge(ldif_ok, 1)
                    act.activation(ltanh[:, :, :], ldif[:, :, :], ACT.Tanh, scale=0.5).then_inc(ltanh_ok, 1)
            for half, tiles in ((0, slice(0, HT)), (1, slice(HT, HT + HT // 2))):
                act.wait_ge(back_mm, half + 1)
                act.copy(o_sb[:, tiles, :], tiled(bank[0:PT, half, :])[:, 0:tiles.stop - tiles.start]).then_inc(o_s, 1)

        @block.vector
        def _(ve):
            count = [0]

            def mark(instruction):
                count[0] += 1
                instruction.then_inc(dve, 1)

            def settle():
                ve.wait_ge(dve, count[0])

            def link(instruction):
                mark(instruction)
                settle()

            ve.memset(filler[:, :], 0.0).then_inc(warm_ok, 1)

            def moments(src, half):
                for i in range(HT):
                    ve.bn_stats(stat[:, half * HT + i, :], src[:, i, :]).then_inc(stat_ok, 1)

            def normalise(src, times):
                ve.wait_ge(stat_ok, NT * (times + 1))
                for i in range(NT):
                    mark(ve.bn_aggr(mv[:, i, :], stat[:, i, :]))
                settle()
                link(ve.tensor_scalar(var[:, :], mv[:, :, 1], EPS, None, ALU.add))
                link(ve.tensor_scalar(rs_a[:, :].bitcast(I32), var[:, :].bitcast(I32), -0.5, GUESS, ALU.mult, ALU.add))
                link(ve.tensor_tensor(rs_b[:, :], rs_a[:, :], rs_a[:, :], ALU.mult))
                link(ve.scalar_tensor_tensor(out=rs_b[:, :], in0=rs_b[:, :], scalar=-STEP_A, in1=var[:, :],
                                             op0=ALU.mult, op1=ALU.mult))
                link(ve.scalar_tensor_tensor(out=rs_c[:, :], in0=rs_b[:, :], scalar=STEP_B, in1=rs_a[:, :],
                                             op0=ALU.add, op1=ALU.mult))
                link(ve.tensor_tensor(rs_b[:, :], rs_c[:, :], rs_c[:, :], ALU.mult))
                link(ve.tensor_tensor(rs_b[:, :], rs_b[:, :], var[:, :], ALU.mult))
                link(ve.tensor_scalar(rs_d[:, :], rs_b[:, :], 0.375, -1.25, ALU.mult, ALU.add))
                link(ve.tensor_tensor(rs_d[:, :], rs_d[:, :], rs_b[:, :], ALU.mult))
                link(ve.scalar_tensor_tensor(out=rstd[:, :], in0=rs_d[:, :], scalar=1.875, in1=rs_c[:, :],
                                             op0=ALU.add, op1=ALU.mult))
                ve.scalar_tensor_tensor(out=shift[:, :], in0=mv[:, :, 0], scalar=-1.0, in1=rstd[:, :],
                                        op0=ALU.mult, op1=ALU.mult).then_inc(norm_ok, 1)
                if times == 1:
                    ve.wait_ge(x2_ok, 2)
                for i in range(NT):
                    if i not in BY_SCALAR[times]:
                        ve.tensor_scalar(xn[:, i, :], src[:, i, :], mv[:, i, 0:1], rstd[:, i:i + 1],
                                         ALU.subtract, ALU.mult).then_inc(xn_v, 1)

            for t in range(2):
                ve.memset(corr_sb[:, t, L:LF], FILL)
            for half in range(2):
                ve.wait_ge(in_x[half], 16)
                moments(x_sb[:, half * HT:(half + 1) * HT, :], half)
            normalise(x_sb, 0)
            def multiply(a, pair, products, multiplied):
                kinds = pair.shape[1]
                return ve.tensor_tensor(products, a.unsqueeze(1).broadcast_to([D, kinds, HS]), pair, ALU.mult).then_inc(multiplied, 1)

            ve.wait_ge(x_spec, 1)
            ve.tensor_copy(xf[:, 0, :], bank[:, 2, 0:HS]).then_inc(xf_ok[0], 1)
            for half in range(2):
                ve.wait_ge(q_proj, half + 1)
                ve.wait_ge(k_ok, half + 1)
                multiply(bank[:, half, 0:HS], kf[:, half, :, :], prod[:, half, :, :], qk_mul)
            ve.wait_ge(qk_mul, 2)
            add_products(ve, prod[:, 1, :, :], qk[:, 1, :], qk_ok[1])
            for half in range(2):
                ve.wait_ge(heads, half + 1)
                tiles = slice(half * HT, (half + 1) * HT)
                ve.tensor_tensor(rsb[:, tiles, :].rearrange("p i (n h) -> p i n h", n=2),
                                 bank[0:PS, 2 + half, 0:HT * NH].rearrange("p (i h) -> p i h", h=NH)
                                 .unsqueeze(2).broadcast_to([PS, HT, 2, NH]),
                                 tb[0:PS, B_MASK:B_MASK + 2 * NH].rearrange("p (n h) -> p n h", n=2)
                                 .unsqueeze(1).broadcast_to([PS, HT, 2, NH]), ALU.mult).then_inc(rsb_ok, 1)
            for t in range(2):
                ve.wait_ge(corr, t + 1)
                mark(ve.max(top8[:, t, :], bank[:, 4 + t, 0:L]))
                mark(ve.tensor_copy(corr_sb[:, t, 0:L], bank[:, 4 + t, 0:L]))
            settle()
            for t in range(2):
                ve.tensor_scalar(ntop[:, t:t + 1], top8[:, t, 0:1], -1.0, None, ALU.mult).then_inc(ntop_ok, 1)
            mark(ve.memset(top8[:, :, TOP:8], FILL))
            settle()
            for t in range(2):
                mark(ve.match_replace(taken[:, t, :], top8[:, t, :], corr_sb[:, t, :], TAKEN))
            settle()
            for t in range(2):
                ve.wait_ge(cexp_ok, t + 1)
                ve.scalar_tensor_tensor(out=wraw[:, t, :], in0=taken[:, t, 0:L], scalar=TAKEN, in1=cexp[:, t, :],
                                        op0=ALU.is_equal, op1=ALU.mult).then_inc(wraw_ok, 1)
            ve.wait_ge(wraw_ok, 2)
            link(ve.tensor_reduce(wsum[:, :], wraw[:, :, :], AX.X, ALU.add))
            mark(ve.reciprocal(winv[:, :], wsum[:, :]))
            for t in range(2):
                ve.wait_ge(wt_mm, t + 1)
                ve.tensor_copy(wtau_t[:, t, :], bank[0:L, t, 0:D]).then_inc(wt_ok, 1)
            settle()
            for t in range(2):
                ve.wait_ge(ws_mm, t + 1)
                ve.scalar_tensor_tensor(out=wown[:, t, :, :], in0=bank[:, 4 + t, 0:SP].unsqueeze(1).broadcast_to([D, NT, SP]),
                                        scalar=winv[:, t:t + 1],
                                        in1=tb[:, B_OWN:B_OWN + NT].unsqueeze(2).broadcast_to([D, NT, SP]),
                                        op0=ALU.mult, op1=ALU.mult).then_inc(wown_ok, 1)
            for half in range(2):
                ve.wait_ge(wrep, half + 1)
                ve.wait_ge(v_ok, half + 1)
                for kind in range(2):
                    multiply(bank[:, 2 + half, 0:HS], vf[:, half, kind:kind + 1, :], tw[:, half, kind:kind + 1, :], of_mul)
                ve.wait_ge(of_mul, 2 * half + 2)
                add_products(ve, tw[:, half, :, :], of[:, half, :], of_ok[half], kinds=(1,))
            for half in range(2):
                ve.wait_ge(attn, half + 1)
                moments(tiled(bank[0:PT, half, :]), half)
            ve.wait_ge(x_spec, 2)
            normalise(x2, 1)
            for half in range(2):
                ve.wait_ge(xth_ok, half + 1)
                ve.tensor_tensor(xtl[:, half, :], bank[:, 6 + half, 0:TOK], xth[:, half, :].bitcast(F32), ALU.subtract).then_inc(xt_ok, 1)

            def logit_differences():
                ve.wait_ge(in_shared, 16)
                ve.wait_ge(logit_mm, 1)
                link(ve.tensor_tensor(logit[:, :, :], bank[0:PT, 4, 0:NT * E].rearrange("p (i e) -> p i e", e=E),
                                      rstd[:, :].unsqueeze(2).broadcast_to([PT, NT, E]), ALU.mult))
                link(ve.tensor_tensor(logit[:, :, :], logit[:, :, :], shared[:, D:D + E].unsqueeze(1).broadcast_to([PT, NT, E]), ALU.add))
                for i in range(NT):
                    mark(ve.max(ltop[:, i, :], logit[:, i, :]))
                settle()
                ve.tensor_tensor(ldif[:, :, :], ltop[:, :, 0:1].broadcast_to([PT, NT, E]), logit[:, :, :],
                                 ALU.subtract).then_inc(ldif_ok, 1)
                mark(ve.tensor_tensor(lmask[:, :, :], logit[:, :, :], ltop[:, :, 1:2].broadcast_to([PT, NT, E]), ALU.is_ge))

            def routes():
                ve.wait_ge(ltanh_ok, 1)
                mark(ve.tensor_scalar(lnum[:, :, :], ltanh[:, :, :], -1.0, 1.0, ALU.mult, ALU.add))
                link(ve.tensor_scalar(lden[:, :, :], ltanh[:, :, :], 1.0, None, ALU.add))
                link(ve.reciprocal(lrec[:, :, :], lden[:, :, :]))
                link(ve.tensor_tensor(lexp[:, :, :], lnum[:, :, :], lrec[:, :, :], ALU.mult))
                link(ve.tensor_tensor(lexp[:, :, :], lexp[:, :, :], lmask[:, :, :], ALU.mult))
                link(ve.tensor_reduce(lsum[:, :], lexp[:, :, :], AX.X, ALU.add))
                link(ve.reciprocal(linv[:, :], lsum[:, :]))
                ve.scalar_tensor_tensor(out=route[:, :, :], in0=lexp[:, :, :], scalar=tanh_g[0:PT, 1:2],
                                        in1=linv[:, :].unsqueeze(2).broadcast_to([PT, NT, E]),
                                        op0=ALU.mult, op1=ALU.mult).then_inc(route_ok, 1)

            def take_expert(e, half):
                if e < E - 1:
                    ve.wait_ge(y_expert, HC * (e + 1))
                    if e >= 2:
                        ve.wait_ge(acc_ok, 2 * (e - 2) + half + 1)
                else:
                    ve.wait_ge(last_half, half + 1)
                    ve.wait_ge(acc_ok, 2 * (e - 2) + half + 1)
                ve.wait_ge(in_route[e], 16)
                into = acc if e == 0 else scaled
                ve.scalar_tensor_tensor(out=into[:, half, :], in0=bank[:, 6 - 2 * (e % 2) + half, 0:TOK],
                                        scalar=col_sb[:, P_B2 + e:P_B2 + e + 1], in1=route_b[:, e % ROUTES, half, :],
                                        op0=ALU.add, op1=ALU.mult).then_inc(scaled_ok, 1)

            takes = {HC * (e + 1) + 1 + half: [(e, half)] for e in range(1, E - 2) for half in range(2)}
            takes.update({2 * HC - 1: [(0, 0)], 2 * HC: [(0, 1)], HC * (E - 1) + 1: [(E - 2, 0), (E - 2, 1)]})
            for n in range(E * HC):
                for part, halves in parts(n):
                    ve.wait_ge(hid_hi, upto(n, part))
                    if n >= SLOTS:
                        ve.wait_ge(y_expert, n - SLOTS + 1)
                    ve.tensor_tensor(hidl[:, n % SLOTS, halves, :], hid[:, n % 2, halves, :],
                                     hidh[:, n % SLOTS, halves, :].bitcast(F32), ALU.subtract).then_inc(hid_ok, 1)
                if n == 0:
                    logit_differences()
                if n == 2:
                    routes()
                if n == 3:
                    for half in range(2):
                        ve.wait_ge(route_mm, half + 1)
                        ve.tensor_copy(route_t[:, half, :], bank[0:E, 4 + half, 0:TOK]).then_inc(route_sb, 1)
                for e, half in takes.get(n, ()):
                    take_expert(e, half)
            for half in range(2):
                take_expert(E - 1, half)
            for half in range(2):
                ve.wait_ge(scaled_ok, 2 * (E - 1) + half + 1)
                ve.wait_ge(acc_ok, 2 * (E - 2))
                ve.tensor_tensor(acc[:, half, 0:TOK // 2], acc[:, half, 0:TOK // 2], scaled[:, half, 0:TOK // 2], ALU.add).then_inc(sum_v, 1)
            ve.wait_ge(back_mm, 3)
            ve.tensor_copy(o_sb[:, HT + HT // 2:, :], tiled(bank[0:PT, 2, :])[:, 0:HT // 2]).then_inc(o_v, 1)

        @block.tensor
        def _(pe):
            def keep_busy(k):
                for _ in range(k):
                    pe.matmul(bank[:, 7, :], filler[:, 0:D], filler[:, :], start=True, stop=True)

            pe.wait_ge(warm_ok, 1)
            keep_busy(FILL_START)

            def to_spectra(src, first, i):
                return pe.matmul(bank[:, first + i // HT, (i % HT) * PS:(i % HT + 1) * PS], src[:, i, :],
                                 ta[:, A_FWD:A_FWD + PS], start=(i % HT == 0), stop=(i % HT == HT - 1),
                                 skip_group_check=True)

            def project_spectra(k, first, src, projected, half):
                pe.matmul(bank[:, first + half, 0:HS], wa_sb[:, k, :], src[:, half, :], start=True, stop=False,
                          skip_group_check=True)
                pe.matmul(spectra(bank[:, first + half, 0:HS])[:, :, 0, 0], rows_sb[:, k, :], ta[0:1, A_DC:A_DC + NT],
                          start=False, stop=True, skip_group_check=True).then_inc(projected, 1)

            for i in range(NT):
                pe.wait_ge(in_c[i // HT], 16)
                mm = to_spectra(c_sb, 0, i)
                if i % HT == HT - 1:
                    mm.then_inc(c_spec, 1)
            pe.wait_ge(in_wa, 16)
            pe.wait_ge(in_rows, 16)
            for half in range(2):
                pe.wait_ge(cf_ok, half + 1)
                project_spectra(1, 4, cf, k_proj, half)
                for i in range(half * HT, (half + 1) * HT):
                    pe.wait_ge(*norm_counts(i, 0))
                    mm = to_spectra(xn, 2, i)
                mm.then_inc(x_spec, 1)
            for half in range(2):
                pe.wait_ge(xf_ok[half], 1)
                project_spectra(0, 0, xf, q_proj, half)
            pe.wait_ge(in_tb, 16)
            for half in range(2):
                project_spectra(2, 6, cf, v_proj, half)
            for half in range(2):
                pe.wait_ge(qk_ok[half], 2)
                for i in range(HT):
                    mm = pe.matmul(bank[0:PS, 2 + half, i * NH:(i + 1) * NH], qk[:, half, i * PS:(i + 1) * PS],
                                   tb[:, B_SUM:B_SUM + NH], start=(i == 0), stop=(i == HT - 1), skip_group_check=True)
                mm.then_inc(heads, 1)
            for t in range(2):
                pe.wait_ge(rsb_ok, t + 1)
                for j in range(HT):
                    mm = pe.matmul(bank[32 * j:32 * j + 32, 4 + t, 0:L], rsb[:, HT * t + j, :], tb[0:PS, B_INV:B_INV + L],
                                   start=True, stop=True, skip_group_check=True, tile_position=(0, 32 * j))
                mm.then_inc(corr, 1)
            pe.wait_ge(centre_ok, 1)
            pe.wait_ge(in_cols, 16)
            pe.wait_ge(v_ok, 1)
            pe.matmul(bank[:, 6, 0:E], centre[:, :], col_sb[:, P_WR:P_WR + E], start=True, stop=True).then_inc(wrc_mm, 1)
            pe.wait_ge(v_ok, 2)
            keep_busy(FILL_TOP)
            for t in range(2):
                pe.wait_ge(wraw_ok, t + 1)
                pe.transpose(bank[0:L, t, 0:D], wraw[:, t, :], ident).then_inc(wt_mm, 1)
            keep_busy(FILL_STEP)
            for t in range(2):
                pe.wait_ge(wt_ok, t + 1)
                pe.matmul(bank[:, 4 + t, 0:SP], wtau_t[:, t, :], tb[0:L, B_FWD1:B_FWD1 + SP], start=True, stop=True).then_inc(ws_mm, 1)
            def add_residual(half):
                pe.wait_ge(xres_ok, 1)
                pe.matmul(bank[0:PT, half, :], ident[0:PT, 0:PT],
                          xres[:, half * HT:(half + 1) * HT, :].rearrange("p i d -> p (i d)"), start=True, stop=False)

            add_residual(0)
            for t in range(2):
                pe.wait_ge(wown_ok, t + 1)
                pe.matmul(bank[:, 2 + t, 0:HS], tb[:, B_REP:B_REP + D], wown[:, t, :, :].rearrange("p b f -> p (b f)"),
                          start=True, stop=True).then_inc(wrep, 1)
            add_residual(1)
            for half in range(2):
                pe.wait_ge(of_ok[half], 2)
                for i in range(HT):
                    mm = pe.matmul(bank[0:PS, 4 + half, i * D:(i + 1) * D], of[:, half, i * PS:(i + 1) * PS], wa_sb[:, 3, :],
                                   start=(i == 0), stop=(i == HT - 1), skip_group_check=True)
                mm.then_inc(y_mm, 1)
            for half in range(2):
                pe.wait_ge(y_ok, half + 1)
                pe.matmul(bank[0:PT, half, :], tb[0:PS, B_OUT:B_OUT + PT],
                          y_sb[:, half * HT:(half + 1) * HT, :].rearrange("p i d -> p (i d)"), start=False, stop=True).then_inc(attn, 1)
            for i in range(NT):
                half = i // HT
                pe.wait_ge(x2_ok, half + 1)
                mm = pe.transpose(bank[:, 4 + half, (i % HT) * PT:(i % HT + 1) * PT], x2[:, i, :], ident[0:PT, 0:PT])
                if i % HT == HT - 1:
                    mm.then_inc(x2t_mm, 1)
            pe.wait_ge(wrc_ok, 1)
            for i in range(NT):
                half, at = i // HT, (i % HT) * PT
                pe.wait_ge(x2t_ok, half + 1)
                mm = pe.matmul(bank[0:PT, 4, i * E:(i + 1) * E], x2t[:, half, at:at + PT], wrc[:, :],
                               start=(i == 0), stop=(i == NT - 1), skip_group_check=True)
            mm.then_inc(logit_mm, 1)
            keep_busy(FILL_NORM)
            for i in range(NT):
                pe.wait_ge(*norm_counts(i, 1))
                mm = pe.transpose(bank[:, 6 + i // HT, (i % HT) * PT:(i % HT + 1) * PT], xn[:, i, :], ident[0:PT, 0:PT])
                if i % HT == HT - 1:
                    mm.then_inc(xt_mm, 1)

            def hidden(n):
                e, c, slot = n // HC, n % HC, n % 2
                if c == 0:
                    pe.wait_ge(we_split, 2 * e + 1)
                if n >= 2:
                    pe.wait_ge(gelu_ok, upto(n - 2))
                cols_ = slice(c * D, (c + 1) * D)
                operands = ((weh, xth), (wel, xth), (weh, xtl))
                for part, halves in parts(n):
                    for k, (w, t) in enumerate(operands):
                        for half in range(halves.start, halves.stop):
                            if n == 0:
                                pe.wait_ge(xt_ok if k == 2 else xth_ok, half + 1)
                            mm = pe.matmul(bank[:, 2 * slot + half, 0:TOK], w[:, e, 0, cols_], t[:, half, :],
                                           start=(k == 0), stop=(k == 2))
                    mm.then_inc(h_mm, 1)

            def turn_routes():
                pe.wait_ge(route_ok, 1)
                for i in range(NT):
                    at = (i % HT) * PT
                    mm = pe.transpose(bank[0:E, 4 + i // HT, at:at + PT], route[:, i, :], ident[0:PT, 0:PT])
                    if i % HT == HT - 1:
                        mm.then_inc(route_mm, 1)

            def project(n):
                e, c, slot = n // HC, n % HC, n % SLOTS
                if c == 0:
                    pe.wait_ge(we_split, 2 * e + 2)
                    if e == 1:
                        pe.wait_ge(route_sb, 2)
                    if e >= 2:
                        pe.wait_ge(scaled_ok, 2 * (e - 1))
                w_of = lambda w: w[:, e, 1, c * D:(c + 1) * D]
                operands = ((weh, hidh), (wel, hidh), (weh, hidl))
                pairs = [(k, half) for k in range(3) for half in range(2)]
                if n == E * HC - 1:
                    pairs = [(k, half) for half in range(2) for k in range(3)]
                for k, half in pairs:
                    pe.wait_ge(hid_ok if k == 2 else hid_hi, upto(n, half if n in IN_HALVES else 0))
                    mm = pe.matmul(bank[:, 6 - 2 * (e % 2) + half, 0:TOK], w_of(operands[k][0]), operands[k][1][:, slot, half, :],
                                   start=(c == 0 and k == 0), stop=(c == HC - 1 and k == 2))
                    if n == E * HC - 1 and k == 2:
                        mm.then_inc(last_half, 1)
                if n < E * HC - 1:
                    mm.then_inc(y_expert, 1)

            hidden(0)
            hidden(1)
            for n in range(E * HC):
                if n + 2 < E * HC:
                    hidden(n + 2)
                if n == 3:
                    turn_routes()
                project(n)
            for place, tiles in enumerate((range(0, HT), range(HT, HT + HT // 2), range(HT + HT // 2, NT))):
                for k, i in enumerate(tiles):
                    half, at = i // HT, (i % HT) * PT
                    pe.wait_ge(sum_v if i % HT < HT // 2 else sum_p, half + 1)
                    mm = pe.transpose(bank[0:PT, place, k * D:(k + 1) * D], acc[:, half, at:at + PT], ident)
                mm.then_inc(back_mm, 1)


def kernel(**inputs):
    import numpy as _np
    import concourse.bacc as _bacc
    from concourse import mybir as _mybir
    from concourse.bass_utils import run_bass_kernel_spmd as _run

    a = {n: _np.asarray(v) for n, v in inputs.items()}
    att, ffn = (lambda n: a["L0_xattn_" + n]), (lambda n: a["L0_ffn_" + n])

    def token_tiles(t):
        return t.reshape(NT, PT, D).transpose(1, 0, 2)

    w1 = ffn("W1").reshape(E, D, 1, H)
    w2 = ffn("W2").reshape(E, HC, D, D).transpose(0, 2, 1, 3).reshape(E, D, 1, H)
    tab_a, tab_b = tables()
    laid = {
        "x": token_tiles(a["x"]),
        "tab_ctx": _np.concatenate([tab_a, token_tiles(a["ctx_1024"][:, :L]).reshape(PT, NT * D)], 1),
        "w_attn": _np.stack([att("Wq"), att("Wk"), att("Wv"), att("Wo")], 1),
        "bias_rows": _np.stack([att("bq"), att("bk"), att("bv")])[None],
        "gates": _np.stack([a["g_xattn"], a["g_ffn"]], 1),
        "shared_rows": _np.concatenate([att("bo"), ffn("br")])[None],
        "cols": _np.concatenate([ffn("b2").T, ffn("b1").reshape(E * HC, D).T, ffn("Wr")], 1),
        "w_experts": _np.concatenate([w1, w2], 2),
        "tab_b": tab_b,
    }
    nc = _bacc.Bacc("TRN2", target_bir_lowering=False, num_devices=1)
    arrays, args = {}, []
    for name, v in laid.items():
        v = _np.ascontiguousarray(v)
        arrays[f"in_{name}"] = v
        args.append(nc.dram_tensor(f"in_{name}", v.shape, _mybir.dt.from_np(v.dtype), kind="ExternalInput").ap())
    out = nc.dram_tensor("out_0", (PT, NT, D), _mybir.dt.float32, kind="ExternalOutput").ap()
    route = nc.dram_tensor("route_scratch", (E, 2, TOK), _mybir.dt.float32, kind="Internal").ap()
    build(nc, *args, out, route)
    got = _run(nc, [arrays], core_ids=[0]).results[0]["out_0"]
    return got.transpose(1, 0, 2).reshape(B, L, D)
```
